# Optimizing a Trainium2 kernel written in Bass

```python
import numpy as np
import jax
import jax.numpy as jnp

def _softmax(x, axis=-1):
    return jax.nn.softmax(x, axis=axis)

def _gelu(x):
    return jax.nn.gelu(x, approximate=True)

def _silu(x):
    return jax.nn.silu(x)

def _sigmoid(x):
    return jax.nn.sigmoid(x)

def _layernorm(x, axis=-1, eps=1e-05):
    m = jnp.mean(x, axis=axis, keepdims=True)
    v = jnp.var(x, axis=axis, keepdims=True)
    return (x - m) / jnp.sqrt(v + eps)

def _scatter_add(tgt, idx, src, axis=0):
    return tgt.at[idx].add(src)

def _segment_sum(src, seg, n):
    return jax.ops.segment_sum(src, seg, n)
kernel_name = 'mk_audio_tower_d1_tok_audfeat2048_r4_8f3ddb'

def setup_inputs(seed: int=0):
    np.random.seed(seed)
    _w = jnp.asarray

    def _rec_inputs():
        import jax
        import jax.numpy as jnp
        _rk = jax.random.key(seed)
        x = -0.000392918 + 0.999932 * jax.random.normal(jax.random.fold_in(_rk, 1), (128, 375, 64), jnp.float32)
        return x
    x = _rec_inputs()

    def _L0_tok_setup():
        import jax, jax.numpy as jnp
        import numpy as np
        TIN = 16
        FEAT = 64
        IN_DIM = TIN * FEAT
        HDIM = 512
        EPS = 1e-06

        def layer_norm(x, gamma, beta, eps):
            mu = jnp.mean(x, axis=-1, keepdims=True)
            var = jnp.mean(jnp.square(x - mu), axis=-1, keepdims=True)
            return (x - mu) * jax.lax.rsqrt(var + eps) * gamma + beta
        key = jax.random.key(seed)
        ks = jax.random.split(key, 4)
        x = jax.random.normal(ks[0], (64, 1024, FEAT), dtype=jnp.float32)
        W = jax.random.normal(ks[1], (IN_DIM, HDIM), dtype=jnp.float32) / np.sqrt(IN_DIM)
        b = jnp.zeros((HDIM,), dtype=jnp.float32)
        g1 = jnp.ones((IN_DIM,), dtype=jnp.float32)
        b1 = jnp.zeros((IN_DIM,), dtype=jnp.float32)
        g2 = jnp.ones((HDIM,), dtype=jnp.float32)
        b2 = jnp.zeros((HDIM,), dtype=jnp.float32)
        return {'x': x, 'W': W, 'b': b, 'g1': g1, 'b1': b1, 'g2': g2, 'b2': b2}
    _L0_tok_all = _L0_tok_setup()
    _L0_tok_in = {k: v for k, v in _L0_tok_all.items() if k in ('W', 'b', 'g1', 'b1', 'g2', 'b2')}
    del _L0_tok_all

    def _L0_attn_setup():
        import jax, jax.numpy as jnp
        import numpy as np
        N_EMBED = 512
        N_HEAD = 16
        N_GROUP = 4
        D_HEAD = N_EMBED // N_HEAD
        GROUP_SIZE = N_HEAD // N_GROUP
        SLIDING_WINDOW = 128
        ATTENTION_SINK = 4
        POS = 0
        ROPE_BASE = 10000.0

        def _rope(x, pos):
            B, T, H, d = x.shape
            half = d // 2
            inv_freq = 1.0 / ROPE_BASE ** (jnp.arange(half, dtype=jnp.float32) * 2.0 / d)
            t = jnp.arange(T, dtype=jnp.float32) + pos
            ang = t[:, None] * inv_freq[None, :]
            cos = jnp.cos(ang)[None, :, None, :].astype(x.dtype)
            sin = jnp.sin(ang)[None, :, None, :].astype(x.dtype)
            x1, x2 = (x[..., :half], x[..., half:])
            return jnp.concatenate([x1 * cos - x2 * sin, x1 * sin + x2 * cos], axis=-1)

        def _sliding_mask(q_len, kv_len):
            i = jnp.arange(q_len)[:, None]
            j = jnp.arange(kv_len)[None, :]
            causal = i >= j
            sink = j < ATTENTION_SINK
            local = j >= i - SLIDING_WINDOW
            return causal & (local | sink)
        key = jax.random.key(seed)
        ks = jax.random.split(key, 9)
        s_in = 1.0 / np.sqrt(N_EMBED)
        x = jax.random.normal(ks[0], (2, 512, N_EMBED), dtype=jnp.float32)
        Wq = jax.random.uniform(ks[1], (N_EMBED, N_HEAD * D_HEAD), jnp.float32, -s_in, s_in)
        bq = jax.random.uniform(ks[2], (N_HEAD * D_HEAD,), jnp.float32, -s_in, s_in)
        Wk = jax.random.uniform(ks[3], (N_EMBED, N_GROUP * D_HEAD), jnp.float32, -s_in, s_in)
        bk = jax.random.uniform(ks[4], (N_GROUP * D_HEAD,), jnp.float32, -s_in, s_in)
        Wv = jax.random.uniform(ks[5], (N_EMBED, N_GROUP * D_HEAD), jnp.float32, -s_in, s_in)
        bv = jax.random.uniform(ks[6], (N_GROUP * D_HEAD,), jnp.float32, -s_in, s_in)
        Wo = jax.random.uniform(ks[7], (N_EMBED, N_EMBED), jnp.float32, -s_in, s_in)
        bo = jax.random.uniform(ks[8], (N_EMBED,), jnp.float32, -s_in, s_in)
        return {'x': x, 'Wq': Wq, 'bq': bq, 'Wk': Wk, 'bk': bk, 'Wv': Wv, 'bv': bv, 'Wo': Wo, 'bo': bo}
    _L0_attn_all = _L0_attn_setup()
    _L0_attn_in = {k: v for k, v in _L0_attn_all.items() if k in ('Wq', 'bq', 'Wk', 'bk', 'Wv', 'bv', 'Wo', 'bo')}
    del _L0_attn_all

    def _L0_ffn_setup():
        import jax, jax.numpy as jnp
        import numpy as np
        NBITS = 4
        OUT_F = 512
        IN_F = 512

        def _bit_ste(w, nbits):
            step = float(2 ** nbits - 1)
            w = jnp.clip(w, -1.0, 1.0)
            return jnp.round(jnp.abs(w) * step) / step * jnp.sign(w)
        key = jax.random.key(seed)
        ks = jax.random.split(key, 6)
        ex = np.arange(NBITS - 1, -1, -1)
        exps = jnp.asarray(2.0 ** ex / (2.0 ** NBITS - 1), dtype=jnp.float32)
        inp = {'input': jax.random.normal(ks[0], (8, 512, IN_F), dtype=jnp.float32), 'pweight': jax.random.normal(ks[1], (OUT_F, IN_F, NBITS), dtype=jnp.float32), 'nweight': jax.random.normal(ks[2], (OUT_F, IN_F, NBITS), dtype=jnp.float32), 'exps': exps, 'bexps': exps, 'mask_weight': jnp.ones((NBITS,), dtype=jnp.float32), 'scale': jnp.array([0.05], dtype=jnp.float32), 'pbias': jax.random.uniform(ks[3], (OUT_F, NBITS), dtype=jnp.float32, minval=0.0, maxval=float(2 ** NBITS - 1)) // 1.0 % 2.0, 'nbias': jax.random.uniform(ks[4], (OUT_F, NBITS), dtype=jnp.float32, minval=0.0, maxval=float(2 ** NBITS - 1)) // 1.0 % 2.0, 'biasscale': jnp.array([0.05], dtype=jnp.float32)}
        return inp
    _L0_ffn_all = _L0_ffn_setup()
    _L0_ffn_in = {k: v for k, v in _L0_ffn_all.items() if k in ('pweight', 'nweight', 'exps', 'bexps', 'mask_weight', 'scale', 'pbias', 'nbias', 'biasscale')}
    del _L0_ffn_all
    return {'x': x, 'L0_tok_W': _L0_tok_in['W'], 'L0_tok_b': _L0_tok_in['b'], 'L0_tok_g1': _L0_tok_in['g1'], 'L0_tok_b1': _L0_tok_in['b1'], 'L0_tok_g2': _L0_tok_in['g2'], 'L0_tok_b2': _L0_tok_in['b2'], 'L0_attn_Wq': _L0_attn_in['Wq'], 'L0_attn_bq': _L0_attn_in['bq'], 'L0_attn_Wk': _L0_attn_in['Wk'], 'L0_attn_bk': _L0_attn_in['bk'], 'L0_attn_Wv': _L0_attn_in['Wv'], 'L0_attn_bv': _L0_attn_in['bv'], 'L0_attn_Wo': _L0_attn_in['Wo'], 'L0_attn_bo': _L0_attn_in['bo'], 'L0_ffn_pweight': _L0_ffn_in['pweight'], 'L0_ffn_nweight': _L0_ffn_in['nweight'], 'L0_ffn_exps': _L0_ffn_in['exps'], 'L0_ffn_bexps': _L0_ffn_in['bexps'], 'L0_ffn_mask_weight': _L0_ffn_in['mask_weight'], 'L0_ffn_scale': _L0_ffn_in['scale'], 'L0_ffn_pbias': _L0_ffn_in['pbias'], 'L0_ffn_nbias': _L0_ffn_in['nbias'], 'L0_ffn_biasscale': _L0_ffn_in['biasscale']}

def reference(x, L0_tok_W, L0_tok_b, L0_tok_g1, L0_tok_b1, L0_tok_g2, L0_tok_b2, L0_attn_Wq, L0_attn_bq, L0_attn_Wk, L0_attn_bk, L0_attn_Wv, L0_attn_bv, L0_attn_Wo, L0_attn_bo, L0_ffn_pweight, L0_ffn_nweight, L0_ffn_exps, L0_ffn_bexps, L0_ffn_mask_weight, L0_ffn_scale, L0_ffn_pbias, L0_ffn_nbias, L0_ffn_biasscale):
    import jax
    import jax.numpy as jnp

    def _L0_tok_ref(x, W, b, g1, b1, g2, b2):
        import jax, jax.numpy as jnp
        import numpy as np
        TIN = 16
        FEAT = 64
        IN_DIM = TIN * FEAT
        HDIM = 512
        EPS = 1e-06

        def layer_norm(x, gamma, beta, eps):
            mu = jnp.mean(x, axis=-1, keepdims=True)
            var = jnp.mean(jnp.square(x - mu), axis=-1, keepdims=True)
            return (x - mu) * jax.lax.rsqrt(var + eps) * gamma + beta
        bsz, T, F = x.shape
        n_patch = T // TIN
        x = x[:, :n_patch * TIN, :].reshape(bsz, n_patch, TIN * F)
        x = layer_norm(x, g1, b1, EPS)
        x = jnp.einsum('bpd,dh->bph', x, W) + b
        return layer_norm(x, g2, b2, EPS)

    def _L0_attn_ref(x, Wq, bq, Wk, bk, Wv, bv, Wo, bo):
        import jax, jax.numpy as jnp
        import numpy as np
        N_EMBED = 512
        N_HEAD = 16
        N_GROUP = 4
        D_HEAD = N_EMBED // N_HEAD
        GROUP_SIZE = N_HEAD // N_GROUP
        SLIDING_WINDOW = 128
        ATTENTION_SINK = 4
        POS = 0
        ROPE_BASE = 10000.0

        def _rope(x, pos):
            B, T, H, d = x.shape
            half = d // 2
            inv_freq = 1.0 / ROPE_BASE ** (jnp.arange(half, dtype=jnp.float32) * 2.0 / d)
            t = jnp.arange(T, dtype=jnp.float32) + pos
            ang = t[:, None] * inv_freq[None, :]
            cos = jnp.cos(ang)[None, :, None, :].astype(x.dtype)
            sin = jnp.sin(ang)[None, :, None, :].astype(x.dtype)
            x1, x2 = (x[..., :half], x[..., half:])
            return jnp.concatenate([x1 * cos - x2 * sin, x1 * sin + x2 * cos], axis=-1)

        def _sliding_mask(q_len, kv_len):
            i = jnp.arange(q_len)[:, None]
            j = jnp.arange(kv_len)[None, :]
            causal = i >= j
            sink = j < ATTENTION_SINK
            local = j >= i - SLIDING_WINDOW
            return causal & (local | sink)
        B, T, C = x.shape
        scale = D_HEAD ** (-0.5)
        Q = (x @ Wq + bq).reshape(B, T, N_HEAD, D_HEAD)
        K = (x @ Wk + bk).reshape(B, T, N_GROUP, D_HEAD)
        V = (x @ Wv + bv).reshape(B, T, N_GROUP, D_HEAD)
        Q = _rope(Q, POS)
        K = _rope(K, POS)
        Q = Q.transpose(0, 2, 1, 3).reshape(B, N_GROUP, GROUP_SIZE, T, D_HEAD)
        K = K.transpose(0, 2, 1, 3)
        V = V.transpose(0, 2, 1, 3)
        scores = jnp.einsum('bghtd,bgsd->bghts', Q, K) * scale
        mask = _sliding_mask(T, T)[None, None, None, :, :]
        neg = jnp.finfo(scores.dtype).min
        scores = jnp.where(mask, scores, neg)
        W = jax.nn.softmax(scores, axis=-1)
        out = jnp.einsum('bghts,bgsd->bghtd', W, V)
        out = out.reshape(B, N_HEAD, T, D_HEAD).transpose(0, 2, 1, 3).reshape(B, T, C)
        return out @ Wo + bo

    def _L0_ffn_ref(input, pweight, nweight, exps, bexps, mask_weight, scale, pbias, nbias, biasscale):
        import jax, jax.numpy as jnp
        import numpy as np
        NBITS = 4
        OUT_F = 512
        IN_F = 512

        def _bit_ste(w, nbits):
            step = float(2 ** nbits - 1)
            w = jnp.clip(w, -1.0, 1.0)
            return jnp.round(jnp.abs(w) * step) / step * jnp.sign(w)
        temp = 1.0
        mask = jax.nn.sigmoid(mask_weight)
        soft = jax.nn.sigmoid(temp * pweight) - jax.nn.sigmoid(temp * nweight)
        weight = jnp.einsum('oin,n->oi', soft, exps * mask) * scale[0]
        bias_raw = jnp.einsum('on,n->o', pbias - nbias, bexps)
        bias = _bit_ste(bias_raw, NBITS) * biasscale[0]
        return jnp.einsum('bsi,oi->bso', input, weight) + bias
    h = _L0_tok_ref(x, L0_tok_W, L0_tok_b, L0_tok_g1, L0_tok_b1, L0_tok_g2, L0_tok_b2)
    h = h + _L0_attn_ref(_layernorm(h, axis=-1), L0_attn_Wq, L0_attn_bq, L0_attn_Wk, L0_attn_bk, L0_attn_Wv, L0_attn_bv, L0_attn_Wo, L0_attn_bo)
    h = h + _L0_ffn_ref(_layernorm(h, axis=-1), L0_ffn_pweight, L0_ffn_nweight, L0_ffn_exps, L0_ffn_bexps, L0_ffn_mask_weight, L0_ffn_scale, L0_ffn_pbias, L0_ffn_nbias, L0_ffn_biasscale)
    return h

_drawn_inputs = setup_inputs


def setup_inputs(seed=0):
    import zlib

    import numpy as np

    out = dict(_drawn_inputs(seed))
    spreads = {'L0_tok_b': (0.0, 0.1),
     'L0_tok_g1': (1.0, 0.2),
     'L0_tok_b1': (0.0, 0.1),
     'L0_tok_g2': (1.0, 0.2),
     'L0_tok_b2': (0.0, 0.1),
     'L0_ffn_mask_weight': (1.0, 0.6)}
    factors = {'L0_attn_bq': 39.644,
     'L0_attn_bk': 64.0,
     'L0_attn_bv': 3.972,
     'L0_ffn_bexps': 3.896,
     'L0_ffn_pbias': 4.248,
     'L0_ffn_nbias': 3.903}
    for name, (base, spread) in spreads.items():
        noise = np.random.default_rng([zlib.crc32(name.encode()), seed]).standard_normal(out[name].shape)
        drawn = base * np.exp(spread * noise) if base else spread * noise
        out[name] = jnp.asarray(drawn.astype(out[name].dtype))
    for name, factor in factors.items():
        out[name] = (out[name] * factor).astype(out[name].dtype)
    return out
```

```python
from contextlib import ExitStack

import numpy as np
import concourse.bass as bass
from concourse import mybir

ALU = mybir.AluOpType
ACT = mybir.ActivationFunctionType
AX_X = mybir.AxisListType.X
F32 = mybir.dt.float32
F32R = mybir.dt.float32r

P = 128
Q = 32
SEQS, FRAMES, FEAT = 128, 375, 64
TIN = 16
IN_DIM = TIN * FEAT
HID = 512
HEADS, GROUPS, HEAD = 16, 4, 32
PER = HEADS // GROUPS
BITS = 4
SEQ = FRAMES // TIN
BATCH = 16
BATCHES = SEQS // BATCH
TOK = BATCH * SEQ
TILES = [(t, min(P, TOK - t)) for t in range(0, TOK, P)]
NT = len(TILES)
CHUNK = 4
CHUNKS = BATCH // CHUNK
CTOK = CHUNK * SEQ
KX = IN_DIM // P
KH = HID // P
HALF = 4
QKV = 2 + KH
HTOK = TOK // 2
PAD = Q - SEQ
EPS_TOK, EPS_LN = 1e-6, 1e-5
STEP = float(2 ** BITS - 1)
NEG = -3.0e38
ZEROED = 6
ROUND = 1.5 * 2.0 ** 23
SCALE = HEAD ** -0.5


def pieces(j):
    at, end, out = TILES[j][0], TILES[j][0] + TILES[j][1], []
    while at < end:
        n = min(SEQ - at % SEQ, end - at)
        out.append((at - TILES[j][0], at // SEQ, at % SEQ, n))
        at += n
    return out


def audio_tower(nc, x, W, b, g1, b1, g2, b2, Wq, bq, Wk, bk, Wv, bv, Wo, bo, pweight, nweight,
                exps, bexps, mask_weight, scale, pbias, nbias, biasscale, cos_t, sin_t, causal, out):
    with ExitStack() as ctx:
        def sb(name, shape, dt=F32):
            return ctx.enter_context(nc.sbuf_tensor(name, shape, dt))

        def pb(name):
            return ctx.enter_context(nc.psum_tensor(name, [P, 512], F32))

        def sem(name):
            return ctx.enter_context(nc.semaphore(name))

        w_hi, w_lo = sb("w_hi", [P, KX, HID], F32R), sb("w_lo", [P, KX, HID], F32R)
        wqkv_hi, wqkv_lo = sb("wqkv_hi", [P, KH, QKV * P], F32R), sb("wqkv_lo", [P, KH, QKV * P], F32R)
        wo_hi, wo_lo = sb("wo_hi", [P, KH, HID], F32R), sb("wo_lo", [P, KH, HID], F32R)
        wf_hi, wf_lo = sb("wf_hi", [P, KH, HID], F32R), sb("wf_lo", [P, KH, HID], F32R)
        y_bias, g2_all, b2_all = sb("y_bias", [P, HID]), sb("g2_all", [P, HID]), sb("b2_all", [P, HID])
        bo_all, f_bias = sb("bo_all", [P, HID]), sb("f_bias", [P, HID])
        mask = sb("mask", [P, SEQ])
        cos, sin = sb("cos", [P, SEQ]), sb("sin", [P, SEQ])
        ident = sb("ident", [P, P])
        qkv_bias = sb("qkv_bias", [P, QKV])
        minus_half = sb("minus_half", [P, 1])
        x_bank = [pb("x_bank0"), pb("x_bank1")]
        turn_bank = pb("turn_bank")
        acc = [pb("acc0"), pb("acc1")]
        s_bank = [pb("s_bank0"), pb("s_bank1")]
        o_bank = pb("o_bank")

        x_loaded = [sem(f"x_loaded{j}") for j in range(NT)]
        (x_moments, x_rstd, x_normed, x_turned, xT_hi_s, xT_lo_s, x_used) = map(sem, (
            "x_moments", "x_rstd", "x_normed", "x_turned", "xT_hi", "xT_lo", "x_used"))
        (y_out, y_moments, y_rstd, y_normed, h_gained, h_ready) = map(sem, (
            "y_out", "y_moments", "y_rstd", "y_normed", "h_gained", "h_ready"))
        (h_moments, h_rstd, h_normed, h_turned, hT_hi_s, hT_lo_s) = map(sem, (
            "h_moments", "h_rstd", "h_normed", "h_turned", "hT_hi_s", "hT_lo_s"))
        (qkv_acc, qkv_out, rope_swapped, rope_cos, rope_sin, roped, k_spread) = map(sem, (
            "qkv_acc", "qkv_out", "rope_swapped", "rope_cos", "rope_sin", "roped", "k_spread"))
        (v_turned, v_spread, s_acc, s_masked, s_max, s_shifted, p_exp, p_sum, p_inv, p_scaled, p_turned) = map(sem, (
            "v_turned", "v_spread", "s_acc", "s_masked", "s_max", "s_shifted", "p_exp", "p_sum", "p_inv",
            "p_scaled", "p_turned"))
        (pv_acc, o_turned, oT_hi_s, oT_lo_s, wo_acc, h_biased, h2_ready, h2_moments, h2_rstd, h2_normed) = map(sem, (
            "pv_acc", "o_turned", "oT_hi_s", "oT_lo_s", "wo_acc", "h_biased", "h2_ready", "h2_moments",
            "h2_rstd", "h2_normed"))
        (f_turned, fT_hi_s, fT_lo_s, f_acc, out_biased, out_ready, out_stored) = map(sem, (
            "f_turned", "fT_hi_s", "fT_lo_s", "f_acc", "out_biased", "out_ready", "out_stored"))
        st = {n: sem(f"stats_{n}") for n in ("x", "y", "h", "f")}
        zeroed, chain, waits_passed = sem("zeroed"), sem("chain"), sem("waits_passed")

        def pairs(t):
            return t[:].rearrange("p k n -> p (k n)")

        with ExitStack() as staging:
            def stage(name, shape):
                return staging.enter_context(nc.sbuf_tensor(name, shape, F32))

            w_raw = stage("w_raw", [P, KX, HID])
            wqkv_raw = stage("wqkv_raw", [P, KH, QKV * P])
            wo_raw = stage("wo_raw", [P, KH, HID])
            p_raw = stage("p_raw", [P, 2, HID * BITS])
            n_raw = stage("n_raw", [P, 2, HID * BITS])
            wf_rows = stage("wf_rows", [P, KH, HID])
            pbias_all, nbias_all = stage("pbias_all", [P, HID * BITS]), stage("nbias_all", [P, HID * BITS])
            b_all = stage("b_all", [P, HID])
            b1_wide = stage("b1_wide", [P, KX, P])
            g1_col, b1_col = stage("g1_col", [P, KX]), stage("b1_col", [P, KX])
            exps_all, bexps_all = stage("exps_all", [P, BITS]), stage("bexps_all", [P, BITS])
            gate, scales, ones = stage("gate", [P, BITS]), stage("scales", [P, 2]), stage("ones", [P, P])

            small_in, w_in, wqkv_in, wo_in, bias_in = map(sem, ("small_in", "w_in", "wqkv_in", "wo_in", "bias_in"))
            f_in = [sem(f"f_in{o}") for o in range(KH)]
            ident_step, w_hi_s, wqkv_hi_s, wo_hi_s, wf_hi_s, gate_s, f_gated = map(sem, (
                "ident_step", "w_hi_s", "wqkv_hi_s", "wo_hi_s", "wf_hi_s", "gate_s", "f_gated"))
            pre_dve, b1_wide_s, y_const, wf_row, wf_turned = map(sem, (
                "pre_dve", "b1_wide_s", "y_const", "wf_row", "wf_turned"))
            wf_bank = [x_bank[0], x_bank[1], acc[0], acc[1]]

            small = [
                (g1_col[:], g1), (b1_col[:], b1),
                (qkv_bias[:, 0:1], bk),
                (qkv_bias[:, 1:2], bv),
                (qkv_bias[:, 2:QKV], bq),
                (exps_all[:], exps.partition_broadcast(P)), (bexps_all[:], bexps.partition_broadcast(P)),
                (gate[:], mask_weight.partition_broadcast(P)),
                (scales[:, 0:1], scale.partition_broadcast(P)), (scales[:, 1:2], biasscale.partition_broadcast(P)),
                (b_all[:], b.partition_broadcast(P)), (g2_all[:], g2.partition_broadcast(P)),
                (b2_all[:], b2.partition_broadcast(P)), (bo_all[:], bo.partition_broadcast(P)),
                (mask[:], causal), (cos[:], cos_t), (sin[:], sin_t),
            ]

            with nc.Block() as block:
                @block.sync
                def _(sp):
                    sp.dma_start(w_raw[:], W.rearrange("(k p) n -> p k n", p=P)).then_inc(w_in, 16)
                    for o in range(KH):
                        if o >= 2:
                            sp.wait_ge(wf_row, o - 1)
                        rows = slice(o * P, (o + 1) * P)
                        sp.dma_start(p_raw[:, o % 2, :], pweight[rows].rearrange("o i n -> o (i n)")).then_inc(f_in[o], 16)
                        sp.dma_start(n_raw[:, o % 2, :], nweight[rows].rearrange("o i n -> o (i n)")).then_inc(f_in[o], 16)

                @block.scalar
                def _(act):
                    for dst, src in small:
                        act.dma_start(dst, src).then_inc(small_in, 16)
                    act.dma_start(wqkv_raw[:, :, 0:P], Wk.rearrange("(k p) n -> p k n", p=P)).then_inc(wqkv_in, 16)
                    act.dma_start(wqkv_raw[:, :, P:2 * P], Wv.rearrange("(k p) n -> p k n", p=P)).then_inc(wqkv_in, 16)
                    act.dma_start(wqkv_raw[:, :, 2 * P:], Wq.rearrange("(k p) n -> p k n", p=P)).then_inc(wqkv_in, 16)
                    act.dma_start(wo_raw[:], Wo.rearrange("(k p) n -> p k n", p=P)).then_inc(wo_in, 16)
                    act.wait_ge(small_in, 16 * len(small))
                    nc.scalar.activation(gate[:], gate[:], ACT.Sigmoid).then_inc(gate_s, 1)
                    for o in range(KH):
                        act.wait_ge(f_in[o], 32)
                        nc.scalar.activation(p_raw[:, o % 2, :], p_raw[:, o % 2, :], ACT.Sigmoid).then_inc(f_gated, 1)
                        nc.scalar.activation(n_raw[:, o % 2, :], n_raw[:, o % 2, :], ACT.Sigmoid).then_inc(f_gated, 1)
                        if o == 0:
                            act.wait_ge(w_in, 16)
                            for k in range(KX):
                                nc.scalar.activation(w_hi[:, k, :], w_raw[:, k, :], ACT.Copy,
                                                     scale=g1_col[:, k:k + 1]).then_inc(w_hi_s, 1)
                        if o == 1:
                            act.wait_ge(wqkv_in, 48)
                            nc.scalar.activation(pairs(wqkv_hi), pairs(wqkv_raw), ACT.Copy).then_inc(wqkv_hi_s, 1)
                            act.wait_ge(wo_in, 16)
                            nc.scalar.activation(pairs(wo_hi), pairs(wo_raw), ACT.Copy).then_inc(wo_hi_s, 1)
                    act.wait_ge(wf_turned, KH)
                    for k in range(KH):
                        nc.scalar.activation(wf_hi[:, k, :], wf_bank[k][:], ACT.Copy).then_inc(wf_hi_s, 1)

                @block.gpsimd
                def _(pool):
                    nc.gpsimd.memset(ident[:], 0.0).then_inc(ident_step, 1)
                    nc.gpsimd.memset(minus_half[:], -0.5).then_inc(ident_step, 1)
                    pool.wait_ge(ident_step, 2)
                    nc.gpsimd.affine_select(out=ident[:], in_=ident[:], compare_op=ALU.not_equal, fill=1.0, base=0,
                                            pattern=[[-1, P]], channel_multiplier=1).then_inc(ident_step, 1)
                    pool.dma_start(pbias_all[:], pbias.rearrange("o n -> (o n)").partition_broadcast(P)).then_inc(bias_in, 16)
                    pool.dma_start(nbias_all[:], nbias.rearrange("o n -> (o n)").partition_broadcast(P)).then_inc(bias_in, 16)

                @block.tensor
                def _(pe):
                    pe.wait_ge(w_in, 16)
                    pe.wait_ge(b1_wide_s, 1)
                    for k in range(KX):
                        mm = nc.tensor.matmul(s_bank[0][:], b1_wide[:, k, :], w_raw[:, k, :],
                                              start=(k == 0), stop=(k == KX - 1))
                    mm.then_inc(y_const, 1)
                    pe.wait_ge(ident_step, 3)
                    for o in range(KH):
                        pe.wait_ge(wf_row, o + 1)
                        for k in range(KH):
                            mm = nc.tensor.transpose(wf_bank[k][:, o * P:(o + 1) * P],
                                                     wf_rows[:, o, k * P:(k + 1) * P], ident[:])
                        mm.then_inc(wf_turned, 1)

                @block.vector
                def _(dve):
                    steps = [0]

                    def after(ins):
                        steps[0] += 1
                        ins.then_inc(pre_dve, 1)
                        dve.wait_ge(pre_dve, steps[0])

                    dve.wait_ge(small_in, 16 * len(small))
                    nc.vector.tensor_copy(b1_wide[:], b1_col[:].unsqueeze(2).broadcast_to([P, KX, P])).then_inc(b1_wide_s, 1)
                    dve.wait_ge(gate_s, 1)
                    after(nc.vector.tensor_tensor(gate[:], gate[:], exps_all[:], ALU.mult))
                    after(nc.vector.tensor_scalar(gate[:], gate[:], scales[:, 0:1], None, ALU.mult))
                    for o in range(KH):
                        dve.wait_ge(f_gated, 2 * o + 2)
                        p = p_raw[:, o % 2, :]
                        after(nc.vector.tensor_tensor(p, p, n_raw[:, o % 2, :], ALU.subtract))
                        p3 = p.rearrange("p (i n) -> p i n", n=BITS)
                        after(nc.vector.tensor_tensor(p3, p3, gate[:].unsqueeze(1).broadcast_to([P, HID, BITS]), ALU.mult))
                        nc.vector.tensor_reduce(wf_rows[:, o, :], p3, AX_X, ALU.add).then_inc(wf_row, 1)
                        if o == 0:
                            for k in range(KX):
                                dve.wait_ge(w_hi_s, k + 1)
                                nc.vector.scalar_tensor_tensor(
                                    out=w_lo[:, k, :], in0=w_raw[:, k, :], scalar=g1_col[:, k:k + 1],
                                    in1=w_hi[:, k, :].bitcast(F32), op0=ALU.mult, op1=ALU.subtract)
                            dve.wait_ge(y_const, 1)
                            nc.vector.tensor_tensor(y_bias[:], s_bank[0][:], b_all[:], ALU.add)
                        if o == 1:
                            dve.wait_ge(wqkv_hi_s, 1)
                            nc.vector.tensor_tensor(pairs(wqkv_lo), pairs(wqkv_raw), pairs(wqkv_hi).bitcast(F32), ALU.subtract)
                            dve.wait_ge(wo_hi_s, 1)
                            nc.vector.tensor_tensor(pairs(wo_lo), pairs(wo_raw), pairs(wo_hi).bitcast(F32), ALU.subtract)
                    dve.wait_ge(bias_in, 32)
                    after(nc.vector.tensor_tensor(pbias_all[:], pbias_all[:], nbias_all[:], ALU.subtract))
                    d3 = pbias_all[:].rearrange("p (o n) -> p o n", n=BITS)
                    after(nc.vector.tensor_tensor(d3, d3, bexps_all[:].unsqueeze(1).broadcast_to([P, HID, BITS]), ALU.mult))
                    after(nc.vector.tensor_reduce(f_bias[:], d3, AX_X, ALU.add))
                    after(nc.vector.tensor_scalar(f_bias[:], f_bias[:], 1.0, -1.0, ALU.min, ALU.max))
                    after(nc.vector.tensor_scalar(f_bias[:], f_bias[:], STEP, ROUND, ALU.mult, ALU.add))
                    after(nc.vector.tensor_scalar(f_bias[:], f_bias[:], ROUND, 1.0 / STEP, ALU.subtract, ALU.mult))
                    after(nc.vector.tensor_scalar(f_bias[:], f_bias[:], scales[:, 1:2], None, ALU.mult))
                    for k in range(KH):
                        dve.wait_ge(wf_hi_s, k + 1)
                        nc.vector.tensor_tensor(wf_lo[:, k, :], wf_bank[k][:], wf_hi[:, k, :].bitcast(F32), ALU.subtract)

        x_tile = sb("x_tile", [P, 2, IN_DIM])
        act_hi, act_lo = sb("act_hi", [P, 3, HALF, P], F32R), sb("act_lo", [P, 3, HALF, P], F32R)
        h = sb("h", [P, 2, NT, HID])
        norm1, norm2 = sb("norm1", [P, HID]), sb("norm2", [P, HID])
        hT_hi, hT_lo = sb("hT_hi", [P, KH, TOK], F32R), sb("hT_lo", [P, KH, TOK], F32R)
        qk = sb("qk", [P, (1 + KH) * TOK + PAD + 1])
        swapped = sb("swapped", [P, KH * TOK])
        vT = sb("vT", [P, BATCH, Q])
        k_diag = sb("k_diag", [P, GROUPS * PER * HTOK + PAD + 1])
        v_diag = sb("v_diag", [P, CHUNKS, GROUPS, CHUNK, Q])
        score = sb("score", [P, 2, HEADS * SEQ])
        prob = sb("prob", [P, 2, HEADS, Q])
        probT = sb("probT", [P, 2, HEADS, Q])
        oT = sb("oT", [P, GROUPS, CHUNK, Q])
        oT_hi, oT_lo = sb("oT_hi", [P, KH, TOK], F32R), sb("oT_lo", [P, KH, TOK], F32R)
        row_max, row_sum, row_inv = sb("row_max", [P, 2, HEADS]), sb("row_sum", [P, 2, HEADS]), sb("row_inv", [P, 2, HEADS])
        stats = sb("stats", [P, 2, 6])
        stats_of = {n: sb(f"stats_of_{n}", [P, 6]) for n in ("y", "h", "f")}
        mo = {n: sb(f"mo_{n}", [P, 5]) for n in ("x", "y", "h", "f")}

        def need(eng, s, count):
            if not isinstance(count, int) or count > 0:
                eng.wait_ge(s, count)

        def alone(eng):
            eng.sem_inc(waits_passed, 1)

        def wide(t, at, stride, n):
            a = t[:, at:at + 1]
            return bass.AP(a.tensor, a.offset, [list(a.ap[0]), [stride, n], [1, Q]])

        def table(t, n):
            return t[:].unsqueeze(1).broadcast_to([P, n, SEQ])

        def heads_of(t, c):
            return t[:, :, c * CTOK:(c + 1) * CTOK].rearrange("p g (s q) -> p g s q", q=SEQ)

        x_tokens = x.rearrange("b t f -> b (t f)")
        out_tokens = out.rearrange("b t d -> (b t) d")

        def run_steps(eng, step):
            step(0, True, False)
            step(1, True, True)
            with eng.Fori(0, (BATCHES - 2) // 2) as i:
                step(i * 2 + 2, True, True, 0)
                step(i * 2 + 3, True, True, 1)
            step(BATCHES, False, True)

        block = ctx.enter_context(nc.Block())

        @block.sync
        def _(sp):
            def step(s, embed, attend, parity=None):
                par = s % 2 if parity is None else parity
                if embed:
                    for j in range(NT):
                        need(sp, x_turned, 6 * s + 2 * j - 2)
                        alone(sp)
                        for row, seq, tok, n in pieces(j):
                            src = x_tokens[bass.ds(s * BATCH + seq, 1), tok * IN_DIM:(tok + n) * IN_DIM]
                            sp.dma_start(x_tile[row:row + n, (NT * par + j) % 2, :],
                                         src.rearrange("a (t d) -> (a t) d", d=IN_DIM)).then_inc(x_loaded[j], 16)
                if attend:
                    b = s - 1
                    sp.wait_ge(roped, 2 * b + 1)
                    alone(sp)
                    for half in range(2):
                        need(sp, s_acc, CHUNKS * b + 2 * half)
                        for g in range(GROUPS):
                            for e in range(PER):
                                at = (g * PER + e) * HTOK
                                sp.dma_start(k_diag[Q * e:Q * e + Q, at:at + HTOK],
                                             qk[Q * g:Q * g + Q, half * HTOK:(half + 1) * HTOK]).then_inc(k_spread, 16)
                    for j, (t, n) in enumerate(TILES):
                        sp.wait_ge(out_ready, NT * b + j + 1)
                        alone(sp)
                        sp.dma_start(out_tokens[bass.ds(b * TOK + t, n), :], h[0:n, 1 - par, j, :]).then_inc(out_stored, 16)
            run_steps(sp, step)
            sp.wait_ge(out_stored, 16 * NT * BATCHES)

        @block.tensor
        def _(pe):
            def x_turn(s, n):
                j, half = n // 2, n % 2
                par = (NT * parity_of[0] + j) % 2
                pe.wait_ge(x_normed, NT * s + j + 1)
                need(pe, xT_lo_s, 6 * s + n - 1)
                m = TILES[j][1]
                for k in range(HALF):
                    at = (half * HALF + k) * P
                    mm = nc.tensor.transpose(x_bank[half][:, k * P:k * P + m], x_tile[0:m, par, at:at + P], ident[0:m, 0:m])
                mm.then_inc(x_turned, 1)

            def split_product(bank, m, lhs, rhs, first, last, dep=None):
                (lh, ll), (rh, rl) = lhs, rhs
                nc.tensor.matmul(bank, lh, rh, start=first, stop=False)
                nc.tensor.matmul(bank, lh, rl, start=False, stop=False)
                return nc.tensor.matmul(bank, ll, rh, start=False, stop=last)

            def x_product(s, n):
                j, half, slot = n // 2, n % 2, n % 3
                m = TILES[j][1]
                pe.wait_ge(xT_lo_s, 6 * s + n + 1)
                if half == 0:
                    if j == 2:
                        pe.wait_ge(y_out, NT * s + 1)
                    else:
                        need(pe, qkv_out, QKV * (s - 1) + 5 + j)
                for k in range(HALF):
                    kk = half * HALF + k
                    mm = split_product(acc[j % 2][0:m, :], m, (act_hi[:, slot, k, 0:m], act_lo[:, slot, k, 0:m]),
                                       (w_hi[:, kk, :], w_lo[:, kk, :]), kk == 0, kk == KX - 1)
                mm.then_inc(x_used, 1)

            def h_turn(s, j):
                m = TILES[j][1]
                pe.wait_ge(h_normed, NT * s + j + 1)
                if j == 0:
                    need(pe, v_spread, CHUNK * s)
                    need(pe, fT_lo_s, NT * (s - 1))
                else:
                    pe.wait_ge(hT_lo_s, NT * s + j)
                for k in range(KH):
                    mm = nc.tensor.transpose(turn_bank[:, k * P:k * P + m], norm1[0:m, k * P:(k + 1) * P], ident[0:m, 0:m])
                mm.then_inc(h_turned, 1)

            def qkv_block(b, n):
                if n == 0:
                    pe.wait_ge(hT_lo_s, NT * b + NT)
                    pe.wait_ge(y_out, NT * b + NT)
                elif n == 1:
                    pe.wait_ge(y_out, NT * b + NT - 1)
                else:
                    pe.wait_ge(qkv_out, QKV * b + n - 1)
                for k in range(KH):
                    cols = slice(n * P, (n + 1) * P)
                    mm = split_product(acc[n % 2][:, 0:TOK], P, (wqkv_hi[:, k, cols], wqkv_lo[:, k, cols]),
                                       (hT_hi[:, k, :], hT_lo[:, k, :]), k == 0, k == KH - 1)
                mm.then_inc(qkv_acc, 1)

            def v_turn(b):
                pe.wait_ge(qkv_out, QKV * b + 2)
                need(pe, fT_lo_s, NT * b)
                pe.wait_ge(hT_lo_s, NT * b + NT)
                for c in range(CHUNKS):
                    mm = nc.tensor.transpose(turn_bank[:, c * P:(c + 1) * P], 
                                             vT[:, c * CHUNK:(c + 1) * CHUNK, :].rearrange("p s q -> p (s q)"), ident[:])
                mm.then_inc(v_turned, 1)

            def scores(b, c):
                if c == 0:
                    pe.wait_ge(roped, 2 * b + 2)
                if c % 2 == 0:
                    pe.wait_ge(k_spread, 16 * 16 * (2 * b + c // 2 + 1))
                if c < 2:
                    need(pe, out_ready, NT * (b - 1) + 2 + c)
                else:
                    pe.wait_ge(s_masked, CHUNKS * b + c - 1)
                for g in range(GROUPS):
                    for q in range(CHUNK):
                        tok = c * CTOK + q * SEQ
                        key_at = g * PER * HTOK + (c % 2) * CTOK + q * SEQ
                        mm = nc.tensor.matmul(s_bank[c % 2][Q * q:Q * q + Q, g * P:(g + 1) * P],
                                              qk[:, (1 + g) * TOK + tok:(1 + g) * TOK + tok + Q],
                                              wide(k_diag, key_at, HTOK, PER), start=True, stop=True)
                mm.then_inc(s_acc, 1)

            def values(b, c):
                pe.wait_ge(p_turned, CHUNKS * b + c + 1)
                if c == 0:
                    pe.wait_ge(v_spread, CHUNK * (b + 1))
                need(pe, o_turned, CHUNKS * b + c)
                for g in range(GROUPS):
                    mm = nc.tensor.matmul(o_bank[:, g * P:(g + 1) * P],
                                          probT[:, c % 2, g * PER:(g + 1) * PER, :].rearrange("p a q -> p (a q)"),
                                          v_diag[:, c, g, :, :].rearrange("p a d -> p (a d)"), start=True, stop=True)
                mm.then_inc(pv_acc, 1)

            def wo_tile(b, j):
                t, m = TILES[j]
                pe.wait_ge(oT_lo_s, CHUNKS * b + CHUNKS)
                if j < 2:
                    pe.wait_ge(s_masked, CHUNKS * b + 3 + j)
                else:
                    pe.wait_ge(h2_ready, NT * b + 1)
                for k in range(KH):
                    mm = split_product(s_bank[j % 2][0:m, :], m, (oT_hi[:, k, t:t + m], oT_lo[:, k, t:t + m]),
                                       (wo_hi[:, k, :], wo_lo[:, k, :]), k == 0, k == KH - 1)
                mm.then_inc(wo_acc, 1)

            def f_turn(s, b, j, embed):
                m = TILES[j][1]
                pe.wait_ge(h2_normed, NT * b + j + 1)
                if embed:
                    pe.wait_ge(hT_lo_s, NT * s + (2 if j == 0 else 3))
                else:
                    pe.wait_ge(v_spread, CHUNK * s)
                need(pe, fT_lo_s, NT * b + j)
                for k in range(KH):
                    mm = nc.tensor.transpose(turn_bank[:, k * P:k * P + m], norm2[0:m, k * P:(k + 1) * P], ident[0:m, 0:m])
                mm.then_inc(f_turned, 1)

            def f_tile(b, j):
                m = TILES[j][1]
                pe.wait_ge(fT_lo_s, NT * b + j + 1)
                pe.wait_ge(*((h2_ready, NT * b + 2 + j) if j < 2 else (out_ready, NT * b + 1)))
                for k in range(KH):
                    mm = split_product(s_bank[1 - j % 2][0:m, :], m, (act_hi[:, j, k, 0:m], act_lo[:, j, k, 0:m]),
                                       (wf_hi[:, k, :], wf_lo[:, k, :]), k == 0, k == KH - 1)
                mm.then_inc(f_acc, 1)

            parity_of = [0]

            def step(s, embed, attend, parity=None):
                parity_of[0] = s % 2 if parity is None else parity
                b = s - 1
                if attend:
                    for n in range(4):
                        qkv_block(b, n)
                if embed:
                    x_turn(s, 0)
                if attend:
                    qkv_block(b, 4)
                if embed:
                    x_turn(s, 1)
                if attend:
                    qkv_block(b, 5)
                if embed:
                    x_turn(s, 2)
                    x_product(s, 0)
                    x_product(s, 1)
                if attend:
                    v_turn(b)
                    scores(b, 0)
                    scores(b, 1)
                if embed:
                    x_turn(s, 3)
                    x_product(s, 2)
                    x_product(s, 3)
                    h_turn(s, 0)
                if attend:
                    values(b, 0)
                    scores(b, 2)
                if embed:
                    x_turn(s, 4)
                    x_turn(s, 5)
                if attend:
                    values(b, 1)
                    scores(b, 3)
                if embed:
                    x_product(s, 4)
                    x_product(s, 5)
                    h_turn(s, 1)
                if attend:
                    values(b, 2)
                    values(b, 3)
                    for j in range(NT):
                        wo_tile(b, j)
                    f_turn(s, b, 0, embed)
                    f_tile(b, 0)
                if embed:
                    h_turn(s, 2)
                if attend:
                    for j in range(1, NT):
                        f_turn(s, b, j, embed)
                        f_tile(b, j)
            pe.wait_ge(zeroed, ZEROED)
            run_steps(pe, step)

        @block.scalar
        def _(act):
            def split_hi(dst, bank, m):
                return nc.scalar.activation(dst[:, :, 0:m], bank[:].rearrange("p (k t) -> p k t", k=HALF)[:, :, 0:m], ACT.Copy)

            def normalise(dst, src, m, key, ready, count, done):
                act.wait_ge(ready, count)
                nc.scalar.activation(dst, src, ACT.Identity, scale=mo[key][0:m, 3:4], bias=mo[key][0:m, 4:5]).then_inc(done, 1)

            def x_normalise(s, j, par):
                m = TILES[j][1]
                t = x_tile[0:m, (NT * par + j) % 2, :]
                normalise(t, t, m, "x", x_rstd, NT * s + j + 1, x_normed)

            def x_high(s, n):
                act.wait_ge(x_turned, 6 * s + n + 1)
                if n < 3:
                    need(act, f_acc, NT * (s - 2) + NT + n - 2)
                    need(act, x_used, 6 * s - 3 + n)
                else:
                    act.wait_ge(x_used, 6 * s + n - 2)
                split_hi(act_hi[:, n % 3], x_bank[n % 2], TILES[n // 2][1]).then_inc(xT_hi_s, 1)

            def qkv_evacuate(b, n):
                act.wait_ge(qkv_acc, QKV * b + n + 1)
                need(act, s_acc, CHUNKS * b)
                if n == 1:
                    dst = vT[:, :, 0:SEQ]
                    need(act, v_turned, b)
                else:
                    at = max(n - 1, 0) * TOK
                    dst = qk[:, at:at + TOK]
                src = acc[n % 2][:, 0:TOK]
                if n == 1:
                    src = src.rearrange("p (s q) -> p s q", q=SEQ)
                nc.scalar.activation(dst, src, ACT.Identity, bias=qkv_bias[:, n:n + 1]).then_inc(qkv_out, 1)

            def y_normalise(s, j):
                m = TILES[j][1]
                t = h[0:m, par_now[0], j, :]
                normalise(t, t, m, "y", y_rstd, NT * s + j + 1, y_normed)

            def spread_values(b):
                act.wait_ge(v_turned, b + 1)
                need(act, pv_acc, CHUNKS * b)
                for q in range(CHUNK):
                    rows = slice(Q * q, Q * q + Q)
                    nc.scalar.activation(v_diag[rows, :, :, q, :].rearrange("p c g d -> p (c g) d"),
                                         turn_bank[rows, :].rearrange("p (c d) -> p c d", d=Q), ACT.Copy).then_inc(v_spread, 1)

            def exponentials(b, c):
                act.wait_ge(s_shifted, CHUNKS * b + c + 1)
                need(act, p_turned, CHUNKS * b + c - 1)
                nc.scalar.activation(prob[:, c % 2, :, 0:SEQ], score[:, c % 2, :].rearrange("p (a k) -> p a k", k=SEQ),
                                     ACT.Exp, scale=SCALE).then_inc(p_exp, 1)

            def h_normalise(s, j):
                m = TILES[j][1]
                need(act, h_turned, NT * s + j)
                normalise(norm1[0:m, :], h[0:m, par_now[0], j, :], m, "h", h_rstd, NT * s + j + 1, h_normed)

            def h_high(s, j):
                t, m = TILES[j]
                act.wait_ge(h_turned, NT * s + j + 1)
                need(act, qkv_acc, QKV * s)
                split_hi(hT_hi[:, :, t:t + m], turn_bank, m).then_inc(hT_hi_s, 1)

            def o_high(b, c):
                act.wait_ge(o_turned, CHUNKS * b + c + 1)
                need(act, wo_acc, NT * b)
                nc.scalar.activation(heads_of(oT_hi, c), oT[:, :, :, 0:SEQ], ACT.Copy).then_inc(oT_hi_s, 1)

            def f_normalise(b, j):
                m = TILES[j][1]
                need(act, f_turned, NT * b + j)
                normalise(norm2[0:m, :], h[0:m, 1 - par_now[0], j, :], m, "f", h2_rstd, NT * b + j + 1, h2_normed)

            def f_high(s, b, j, embed):
                act.wait_ge(f_turned, NT * b + j + 1)
                if embed:
                    act.wait_ge(x_used, 6 * s + 4 + j)
                else:
                    act.wait_ge(f_acc, NT * (b - 1) + j + 1)
                split_hi(act_hi[:, j], turn_bank, TILES[j][1]).then_inc(fT_hi_s, 1)

            par_now = [0]

            def step(s, embed, attend, parity=None):
                par = par_now[0] = s % 2 if parity is None else parity
                b = s - 1
                if embed:
                    x_normalise(s, 0, par)
                if attend:
                    qkv_evacuate(b, 0)
                    qkv_evacuate(b, 1)
                    qkv_evacuate(b, 2)
                if embed:
                    x_normalise(s, 1, par)
                if attend:
                    qkv_evacuate(b, 3)
                if embed:
                    x_high(s, 0)
                if attend:
                    qkv_evacuate(b, 4)
                if embed:
                    x_high(s, 1)
                if attend:
                    qkv_evacuate(b, 5)
                if embed:
                    x_high(s, 2)
                    y_normalise(s, 0)
                if attend:
                    spread_values(b)
                    exponentials(b, 0)
                if embed:
                    x_high(s, 3)
                if attend:
                    exponentials(b, 1)
                if embed:
                    h_normalise(s, 0)
                    x_normalise(s, 2, par)
                    h_high(s, 0)
                    y_normalise(s, 1)
                if attend:
                    o_high(b, 0)
                    exponentials(b, 2)
                if embed:
                    x_high(s, 4)
                    x_high(s, 5)
                if attend:
                    o_high(b, 1)
                if embed:
                    h_normalise(s, 1)
                if attend:
                    exponentials(b, 3)
                if embed:
                    h_high(s, 1)
                    y_normalise(s, 2)
                if attend:
                    o_high(b, 2)
                    o_high(b, 3)
                if embed:
                    h_normalise(s, 2)
                if attend:
                    f_normalise(b, 0)
                    f_high(s, b, 0, embed)
                    f_normalise(b, 1)
                if embed:
                    h_high(s, 2)
                if attend:
                    f_high(s, b, 1, embed)
                    f_normalise(b, 2)
                    f_high(s, b, 2, embed)
            act.wait_ge(zeroed, ZEROED)
            run_steps(act, step)

        @block.gpsimd
        def _(pool):
            def deviation(key, m, eps, moments, rstd, count):
                v = mo[key]
                pool.wait_ge(moments, count)
                alone(pool)
                nc.gpsimd.tensor_scalar(v[0:m, 2:3], v[0:m, 1:2], eps, None, ALU.add).then_inc(chain, 1)
                tick(1)
                nc.gpsimd.tensor_tensor(v[0:m, 3:4], v[0:m, 2:3], minus_half[0:m, :], ALU.pow).then_inc(chain, 1)
                tick(1)
                alone(pool)
                nc.gpsimd.tensor_scalar(v[0:m, 4:5], v[0:m, 0:1], v[0:m, 3:4], -1.0, ALU.mult, ALU.mult).then_inc(rstd, 1)

            def tick(n):
                done[0] += n
                pool.wait_ge(chain, base[0] + done[0])

            def rope_cosine(b, n):
                at, blocks = (0, 1) if n == 0 else (TOK, KH)
                v = qk[:, at:at + blocks * TOK].rearrange("p (a t) -> p a t", t=SEQ)
                pool.wait_ge(rope_swapped, 2 * b + n + 1)
                nc.gpsimd.tensor_tensor(v, v, table(cos, blocks * BATCH), ALU.mult).then_inc(rope_cos, 1)

            def gain(s, j):
                m = TILES[j][1]
                t = h[0:m, par_now[0], j, :]
                pool.wait_ge(y_normed, NT * s + j + 1)
                nc.gpsimd.tensor_tensor(t, t, g2_all[0:m, :], ALU.mult).then_inc(h_gained, 1)
                pool.wait_ge(h_gained, NT * s + j + 1)
                nc.gpsimd.tensor_tensor(t, t, b2_all[0:m, :], ALU.add).then_inc(h_ready, 1)

            def shift(b, c):
                v = score[:, c % 2, :].rearrange("p (a k) -> p a k", k=SEQ)
                pool.wait_ge(s_max, CHUNKS * b + c + 1)
                nc.gpsimd.tensor_tensor(v, v, row_max[:, c % 2, :].unsqueeze(2).broadcast_to([P, HEADS, SEQ]),
                                        ALU.subtract).then_inc(s_shifted, 1)

            def divide(b, c):
                v = prob[:, c % 2, :, 0:SEQ]
                pool.wait_ge(p_inv, CHUNKS * b + c + 1)
                nc.gpsimd.tensor_tensor(v, v, row_inv[:, c % 2, :].unsqueeze(2).broadcast_to([P, HEADS, SEQ]),
                                        ALU.mult).then_inc(p_scaled, 1)

            def add_output_bias(b, j):
                m = TILES[j][1]
                t = h[0:m, 1 - par_now[0], j, :]
                pool.wait_ge(h_normed, NT * b + j + 1)
                nc.gpsimd.tensor_tensor(t, t, bo_all[0:m, :], ALU.add).then_inc(h_biased, 1)

            def add_ffn_bias(b, j):
                m = TILES[j][1]
                t = h[0:m, 1 - par_now[0], j, :]
                pool.wait_ge(h2_normed, NT * b + j + 1)
                nc.gpsimd.tensor_tensor(t, t, f_bias[0:m, :], ALU.add).then_inc(out_biased, 1)

            par_now, done, base = [0], [0], [0]
            PER_TILE = 2

            def step(s, embed, attend, parity=None):
                par_now[0] = s % 2 if parity is None else parity
                b = s - 1
                done[0] = 0
                base[0] = PER_TILE * NT * 3 * s + (PER_TILE * NT * b if attend else 0)

                def x_dev(j):
                    deviation("x", TILES[j][1], EPS_TOK, x_moments, x_rstd, NT * s + j + 1)

                def y_dev(j):
                    deviation("y", TILES[j][1], EPS_TOK, y_moments, y_rstd, NT * s + j + 1)

                def h_dev(j):
                    deviation("h", TILES[j][1], EPS_LN, h_moments, h_rstd, NT * s + j + 1)

                def f_dev(j):
                    deviation("f", TILES[j][1], EPS_LN, h2_moments, h2_rstd, NT * b + j + 1)

                if embed:
                    x_dev(0)
                if attend:
                    rope_cosine(b, 0)
                if embed:
                    x_dev(1)
                if attend:
                    rope_cosine(b, 1)
                if embed:
                    y_dev(0)
                    gain(s, 0)
                if attend:
                    shift(b, 0)
                    shift(b, 1)
                    divide(b, 0)
                if embed:
                    h_dev(0)
                if attend:
                    divide(b, 1)
                if embed:
                    x_dev(2)
                    y_dev(1)
                    gain(s, 1)
                if attend:
                    shift(b, 2)
                if embed:
                    h_dev(1)
                if attend:
                    divide(b, 2)
                    shift(b, 3)
                    divide(b, 3)
                if embed:
                    y_dev(2)
                    gain(s, 2)
                if attend:
                    for j in range(NT):
                        add_output_bias(b, j)
                if embed:
                    h_dev(2)
                if attend:
                    f_dev(0)
                    f_dev(1)
                    add_ffn_bias(b, 0)
                    f_dev(2)
                    add_ffn_bias(b, 1)
                    add_ffn_bias(b, 2)
            for ap in (qk[:, (1 + KH) * TOK:], vT[:], k_diag[:], v_diag[:], prob[:], swapped[:, 0:1]):
                nc.gpsimd.memset(ap, 0.0).then_inc(zeroed, 1)
            pool.wait_ge(zeroed, ZEROED)
            run_steps(pool, step)

        @block.vector
        def _(dve):
            def moments(key, src, m, done, count):
                n = src.shape[-1] // 512
                for i in range(n):
                    ins = nc.vector.bn_stats(stats[0:m, 0 if key != "x" else i, :] if key == "x" else stats_of[key][0:m, :],
                                             src[:, i * 512:(i + 1) * 512]).then_inc(st[key], 1)
                dve.wait_ge(st[key], count * n)
                src6 = stats[0:m, 0:2, :].rearrange("p a b -> p (a b)") if key == "x" else stats_of[key][0:m, :]
                alone(dve)
                nc.vector.bn_aggr(mo[key][0:m, 0:2], src6).then_inc(done, 1)

            def x_stats(s, j, par):
                m = TILES[j][1]
                dve.wait_ge(x_loaded[j], 16 * len(pieces(j)) * (s + 1))
                need(dve, x_normed, NT * s + j)
                moments("x", x_tile[0:m, (NT * par + j) % 2, :], m, x_moments, NT * s + j + 1)

            def split_lo(dst, bank, hi, m):
                return nc.vector.tensor_tensor(dst[:, :, 0:m], bank[:].rearrange("p (k t) -> p k t", k=HALF)[:, :, 0:m],
                                               hi[:, :, 0:m].bitcast(F32), ALU.subtract)

            def x_low(s, n):
                dve.wait_ge(xT_hi_s, 6 * s + n + 1)
                split_lo(act_lo[:, n % 3], x_bank[n % 2], act_hi[:, n % 3], TILES[n // 2][1]).then_inc(xT_lo_s, 1)

            def rope(b, n):
                at, blocks, first = (0, 1, 0) if n == 0 else (TOK, KH, 2)
                v, w = qk[:, at:at + blocks * TOK], swapped[:, 0:blocks * TOK]
                dve.wait_ge(qkv_out, QKV * b + (1 if n == 0 else QKV))
                need(dve, roped, 2 * b + n)
                alone(dve)
                nc.vector.stream_shuffle(w, v, [(i + HEAD // 2) % Q for i in range(Q)]).then_inc(rope_swapped, 1)
                dve.wait_ge(rope_swapped, 2 * b + n + 1)
                w3 = w.rearrange("p (a t) -> p a t", t=SEQ)
                nc.vector.tensor_tensor(w3, w3, table(sin, blocks * BATCH), ALU.mult).then_inc(rope_sin, 1)
                dve.wait_ge(rope_sin, 2 * b + n + 1)
                dve.wait_ge(rope_cos, 2 * b + n + 1)
                if n == 0:
                    need(dve, k_spread, 16 * 16 * 2 * b)
                nc.vector.tensor_tensor(v, v, w, ALU.add).then_inc(roped, 1)

            def y_evacuate(s, j):
                m = TILES[j][1]
                t = h[0:m, par_now[0], j, :]
                dve.wait_ge(x_used, 6 * s + 2 * j + 2)
                need(dve, out_stored, 16 * (NT * (s - 2) + NT))
                nc.vector.tensor_tensor(t, acc[j % 2][0:m, :], y_bias[0:m, :], ALU.add).then_inc(y_out, 1)
                dve.wait_ge(y_out, NT * s + j + 1)
                need(dve, y_normed, NT * s + j)
                moments("y", t, m, y_moments, NT * s + j + 1)

            def mask_scores(b, c):
                v = score[:, c % 2, :].rearrange("p (a k) -> p a k", k=SEQ)
                dve.wait_ge(s_acc, CHUNKS * b + c + 1)
                need(dve, p_exp, CHUNKS * b + c - 1)
                need(dve, s_shifted, CHUNKS * b + c - 1)
                nc.vector.tensor_tensor(v, s_bank[c % 2][:].rearrange("p (a k) -> p a k", k=Q)[:, :, 0:SEQ],
                                        mask[:].unsqueeze(1).broadcast_to([P, HEADS, SEQ]), ALU.add).then_inc(s_masked, 1)
                dve.wait_ge(s_masked, CHUNKS * b + c + 1)
                nc.vector.tensor_reduce(row_max[:, c % 2, :], v, AX_X, ALU.max).then_inc(s_max, 1)

            def sum_up(b, c):
                dve.wait_ge(p_exp, CHUNKS * b + c + 1)
                need(dve, p_scaled, CHUNKS * b + c - 1)
                nc.vector.tensor_reduce(row_sum[:, c % 2, :], prob[:, c % 2, :, 0:SEQ], AX_X, ALU.add).then_inc(p_sum, 1)
                dve.wait_ge(p_sum, CHUNKS * b + c + 1)
                nc.vector.reciprocal(row_inv[:, c % 2, :], row_sum[:, c % 2, :]).then_inc(p_inv, 1)

            def turn_probs(b, c):
                dve.wait_ge(p_scaled, CHUNKS * b + c + 1)
                need(dve, pv_acc, CHUNKS * b + c - 1)
                nc.vector.transpose(probT[:, c % 2].rearrange("p a q -> p (a q)"),
                                    prob[:, c % 2].rearrange("p a q -> p (a q)")).then_inc(p_turned, 1)

            def turn_heads(b, c):
                dve.wait_ge(pv_acc, CHUNKS * b + c + 1)
                need(dve, oT_hi_s, CHUNKS * b + c)
                need(dve, oT_lo_s, CHUNKS * b + c)
                nc.vector.transpose(oT[:].rearrange("p g s q -> p (g s q)"), o_bank[:]).then_inc(o_turned, 1)

            def o_low(b, c):
                dve.wait_ge(oT_hi_s, CHUNKS * b + c + 1)
                nc.vector.tensor_tensor(heads_of(oT_lo, c), oT[:, :, :, 0:SEQ],
                                        heads_of(oT_hi, c).bitcast(F32), ALU.subtract).then_inc(oT_lo_s, 1)

            def h_stats(s, j):
                m = TILES[j][1]
                dve.wait_ge(h_ready, NT * s + j + 1)
                need(dve, h_normed, NT * s + j)
                moments("h", h[0:m, par_now[0], j, :], m, h_moments, NT * s + j + 1)

            def h_low(s, j):
                t, m = TILES[j]
                dve.wait_ge(hT_hi_s, NT * s + j + 1)
                split_lo(hT_lo[:, :, t:t + m], turn_bank, hT_hi[:, :, t:t + m], m).then_inc(hT_lo_s, 1)

            def add_attention(b, j):
                m = TILES[j][1]
                t = h[0:m, 1 - par_now[0], j, :]
                dve.wait_ge(wo_acc, NT * b + j + 1)
                dve.wait_ge(h_biased, NT * b + j + 1)
                nc.vector.tensor_tensor(t, s_bank[j % 2][0:m, :], t, ALU.add).then_inc(h2_ready, 1)
                dve.wait_ge(h2_ready, NT * b + j + 1)
                need(dve, h2_normed, NT * b + j)
                moments("f", t, m, h2_moments, NT * b + j + 1)

            def f_low(b, j):
                dve.wait_ge(fT_hi_s, NT * b + j + 1)
                split_lo(act_lo[:, j], turn_bank, act_hi[:, j], TILES[j][1]).then_inc(fT_lo_s, 1)

            def add_ffn(b, j):
                m = TILES[j][1]
                t = h[0:m, 1 - par_now[0], j, :]
                dve.wait_ge(f_acc, NT * b + j + 1)
                dve.wait_ge(out_biased, NT * b + j + 1)
                nc.vector.tensor_tensor(t, s_bank[1 - j % 2][0:m, :], t, ALU.add).then_inc(out_ready, 1)

            par_now = [0]

            def step(s, embed, attend, parity=None):
                par = par_now[0] = s % 2 if parity is None else parity
                b = s - 1
                if embed:
                    x_stats(s, 0, par)
                if attend:
                    rope(b, 0)
                if embed:
                    x_stats(s, 1, par)
                    x_low(s, 0)
                    x_low(s, 1)
                if attend:
                    rope(b, 1)
                if embed:
                    x_low(s, 2)
                    y_evacuate(s, 0)
                if attend:
                    mask_scores(b, 0)
                    mask_scores(b, 1)
                if embed:
                    x_low(s, 3)
                if attend:
                    sum_up(b, 0)
                if embed:
                    h_stats(s, 0)
                if attend:
                    turn_probs(b, 0)
                    sum_up(b, 1)
                if embed:
                    x_stats(s, 2, par)
                if attend:
                    turn_probs(b, 1)
                if embed:
                    h_low(s, 0)
                    y_evacuate(s, 1)
                if attend:
                    turn_heads(b, 0)
                    mask_scores(b, 2)
                    o_low(b, 0)
                if embed:
                    x_low(s, 4)
                    x_low(s, 5)
                if attend:
                    turn_heads(b, 1)
                if embed:
                    h_stats(s, 1)
                if attend:
                    sum_up(b, 2)
                    o_low(b, 1)
                    mask_scores(b, 3)
                    turn_probs(b, 2)
                if embed:
                    h_low(s, 1)
                if attend:
                    sum_up(b, 3)
                    turn_probs(b, 3)
                if embed:
                    y_evacuate(s, 2)
                if attend:
                    turn_heads(b, 2)
                    o_low(b, 2)
                    turn_heads(b, 3)
                    o_low(b, 3)
                if embed:
                    h_stats(s, 2)
                if attend:
                    add_attention(b, 0)
                    add_attention(b, 1)
                    f_low(b, 0)
                    add_attention(b, 2)
                if embed:
                    h_low(s, 2)
                if attend:
                    f_low(b, 1)
                    add_ffn(b, 0)
                    f_low(b, 2)
                    add_ffn(b, 1)
                    add_ffn(b, 2)
            dve.wait_ge(zeroed, ZEROED)
            run_steps(dve, step)


_INS = ["x", "L0_tok_W", "L0_tok_b", "L0_tok_g1", "L0_tok_b1", "L0_tok_g2", "L0_tok_b2", "L0_attn_Wq", "L0_attn_bq",
        "L0_attn_Wk", "L0_attn_bk", "L0_attn_Wv", "L0_attn_bv", "L0_attn_Wo", "L0_attn_bo", "L0_ffn_pweight",
        "L0_ffn_nweight", "L0_ffn_exps", "L0_ffn_bexps", "L0_ffn_mask_weight", "L0_ffn_scale", "L0_ffn_pbias",
        "L0_ffn_nbias", "L0_ffn_biasscale"]


def shape_tables():
    inv = 1.0 / 10000.0 ** (np.arange(HEAD // 2, dtype=np.float32) * 2.0 / HEAD)
    angle = inv.astype(np.float32)[:, None] * np.arange(SEQ, dtype=np.float32)[None, :]
    cos, sin = np.cos(angle), np.sin(angle)
    cos = np.tile(np.concatenate([cos, cos]), (P // Q, 1)).astype(np.float32)
    sin = np.tile(np.concatenate([-sin, sin]), (P // Q, 1)).astype(np.float32)
    query, key = np.arange(Q)[:, None], np.arange(SEQ)[None, :]
    causal = np.tile(np.where(key <= query, 0.0, NEG), (P // Q, 1)).astype(np.float32)
    return {"cos": cos, "sin": sin, "causal": causal}


def kernel(**inputs):
    import concourse.bacc as _bacc
    from concourse.bass_utils import run_bass_kernel_spmd as _run

    nc = _bacc.Bacc("TRN2", target_bir_lowering=False, num_devices=1)
    arrays, args = {}, []
    given = {name: np.asarray(inputs[name]) for name in _INS} | shape_tables()
    for name in ("L0_tok_g1", "L0_tok_b1", "L0_attn_bq", "L0_attn_bk", "L0_attn_bv"):
        given[name] = given[name].reshape(-1, P).T
    given = {name: np.ascontiguousarray(a) for name, a in given.items()}
    for name, a in given.items():
        arrays[f"in_{name}_dram"] = a
        args.append(nc.dram_tensor(f"in_{name}_dram", a.shape, mybir.dt.from_np(a.dtype), kind="ExternalInput").ap())
    args.append(nc.dram_tensor("out_0_dram", (SEQS, SEQ, HID), F32, kind="ExternalOutput").ap())
    audio_tower(nc, *args)
    r = _run(nc, [arrays], core_ids=[0])
    return r.results[0]["out_0_dram"]
```

```python
from contextlib import ExitStack

import numpy as np
import concourse.bass as bass
from concourse import mybir

ALU = mybir.AluOpType
ACT = mybir.ActivationFunctionType
AX_X = mybir.AxisListType.X
F32 = mybir.dt.float32
F32R = mybir.dt.float32r

P = 128
Q = 32
SEQS, FRAMES, FEAT = 128, 375, 64
TIN = 16
IN_DIM = TIN * FEAT
HID = 512
HEADS, GROUPS, HEAD = 16, 4, 32
PER = HEADS // GROUPS
BITS = 4
SEQ = FRAMES // TIN
BATCH = 16
BATCHES = SEQS // BATCH
TOK = BATCH * SEQ
TILES = [(t, min(P, TOK - t)) for t in range(0, TOK, P)]
NT = len(TILES)
CHUNK = 4
CHUNKS = BATCH // CHUNK
CTOK = CHUNK * SEQ
KX = IN_DIM // P
KH = HID // P
HALF = 4
QKV = 2 + KH
ROPE = [(0, 1), (1, 2), (3, 2)]
PAD = Q - SEQ
EPS_TOK, EPS_LN = 1e-6, 1e-5
STEP = float(2 ** BITS - 1)
NEG = -3.0e38
ZEROED = 5
ROUND = 1.5 * 2.0 ** 23
SCALE = HEAD ** -0.5


def pieces(j):
    at, end, out = TILES[j][0], TILES[j][0] + TILES[j][1], []
    while at < end:
        n = min(SEQ - at % SEQ, end - at)
        out.append((at - TILES[j][0], at // SEQ, at % SEQ, n))
        at += n
    return out


def audio_tower(nc, x, W, b, g1, b1, g2, b2, Wq, bq, Wk, bk, Wv, bv, Wo, bo, pweight, nweight,
                exps, bexps, mask_weight, scale, pbias, nbias, biasscale, cos_t, sin_t, causal, out):
    with ExitStack() as ctx:
        def sb(name, shape, dt=F32):
            return ctx.enter_context(nc.sbuf_tensor(name, shape, dt))

        def pb(name):
            return ctx.enter_context(nc.psum_tensor(name, [P, 512], F32))

        def sem(name):
            return ctx.enter_context(nc.semaphore(name))

        w_hi, w_lo = sb("w_hi", [P, KX, HID], F32R), sb("w_lo", [P, KX, HID], F32R)
        wqkv_hi, wqkv_lo = sb("wqkv_hi", [P, KH, QKV * P], F32R), sb("wqkv_lo", [P, KH, QKV * P], F32R)
        wo_hi, wo_lo = sb("wo_hi", [P, KH, HID], F32R), sb("wo_lo", [P, KH, HID], F32R)
        wf_hi, wf_lo = sb("wf_hi", [P, KH, HID], F32R), sb("wf_lo", [P, KH, HID], F32R)
        y_bias, g2_all, b2_all = sb("y_bias", [P, HID]), sb("g2_all", [P, HID]), sb("b2_all", [P, HID])
        bo_all, f_bias = sb("bo_all", [P, HID]), sb("f_bias", [P, HID])
        mask = sb("mask", [P, SEQ])
        cos, sin = sb("cos", [P, SEQ]), sb("sin", [P, SEQ])
        ident = sb("ident", [P, P])
        qkv_bias = sb("qkv_bias", [P, QKV])
        minus_half = sb("minus_half", [P, 1])
        x_bank = [pb("x_bank0"), pb("x_bank1")]
        turn_bank = pb("turn_bank")
        acc = [pb("acc0"), pb("acc1")]
        s_bank = [pb("s_bank0"), pb("s_bank1")]
        o_bank = pb("o_bank")

        x_loaded = [sem(f"x_loaded{j}") for j in range(NT)]
        (x_moments, x_rstd, x_normed, x_turned, xT_hi_s, xT_lo_s, x_used) = map(sem, (
            "x_moments", "x_rstd", "x_normed", "x_turned", "xT_hi", "xT_lo", "x_used"))
        (y_out, y_moments, y_rstd, h_gained, h_ready) = map(sem, (
            "y_out", "y_moments", "y_rstd", "h_gained", "h_ready"))
        (h_moments, h_rstd, h_normed, h_turned, hT_hi_s, hT_lo_s) = map(sem, (
            "h_moments", "h_rstd", "h_normed", "h_turned", "hT_hi_s", "hT_lo_s"))
        (qkv_acc, qkv_out, rope_swapped, rope_cos, rope_sin, roped, k_spread) = map(sem, (
            "qkv_acc", "qkv_out", "rope_swapped", "rope_cos", "rope_sin", "roped", "k_spread"))
        (v_turned, v_spread, s_acc, s_masked, s_max, s_shifted, p_exp, p_sum, p_inv, p_scaled, p_turned) = map(sem, (
            "v_turned", "v_spread", "s_acc", "s_masked", "s_max", "s_shifted", "p_exp", "p_sum", "p_inv",
            "p_scaled", "p_turned"))
        (pv_acc, o_turned, oT_hi_s, oT_lo_s, wo_acc, h_biased, h2_ready, h2_moments, h2_rstd, h2_normed) = map(sem, (
            "pv_acc", "o_turned", "oT_hi_s", "oT_lo_s", "wo_acc", "h_biased", "h2_ready", "h2_moments",
            "h2_rstd", "h2_normed"))
        (f_turned, fT_hi_s, fT_lo_s, f_acc, out_biased, out_ready, out_stored) = map(sem, (
            "f_turned", "fT_hi_s", "fT_lo_s", "f_acc", "out_biased", "out_ready", "out_stored"))
        st = {n: sem(f"stats_{n}") for n in ("x", "y", "h", "f")}
        zeroed, chain, waits_passed = sem("zeroed"), sem("chain"), sem("waits_passed")

        def pairs(t):
            return t[:].rearrange("p k n -> p (k n)")

        with ExitStack() as staging:
            def stage(name, shape):
                return staging.enter_context(nc.sbuf_tensor(name, shape, F32))

            w_raw = stage("w_raw", [P, KX, HID])
            wqkv_raw = stage("wqkv_raw", [P, KH, QKV * P])
            wo_raw = stage("wo_raw", [P, KH, HID])
            p_raw = stage("p_raw", [P, 2, HID * BITS])
            n_raw = stage("n_raw", [P, 2, HID * BITS])
            wf_rows = stage("wf_rows", [P, KH, HID])
            pbias_all, nbias_all = stage("pbias_all", [P, HID * BITS]), stage("nbias_all", [P, HID * BITS])
            b_all = stage("b_all", [P, HID])
            b1_wide = stage("b1_wide", [P, KX, P])
            g1_col, b1_col = stage("g1_col", [P, KX]), stage("b1_col", [P, KX])
            exps_all, bexps_all = stage("exps_all", [P, BITS]), stage("bexps_all", [P, BITS])
            gate, scales, ones = stage("gate", [P, BITS]), stage("scales", [P, 2]), stage("ones", [P, P])

            small_in, w_in, wqkv_in, wo_in, bias_in = map(sem, ("small_in", "w_in", "wqkv_in", "wo_in", "bias_in"))
            f_in = [sem(f"f_in{o}") for o in range(KH)]
            ident_step, w_hi_s, wqkv_hi_s, wo_hi_s, wf_hi_s, gate_s, f_gated = map(sem, (
                "ident_step", "w_hi_s", "wqkv_hi_s", "wo_hi_s", "wf_hi_s", "gate_s", "f_gated"))
            pre_dve, b1_wide_s, y_const, wf_row, wf_turned = map(sem, (
                "pre_dve", "b1_wide_s", "y_const", "wf_row", "wf_turned"))
            wf_bank = [x_bank[0], x_bank[1], acc[0], acc[1]]

            small = [
                (g1_col[:], g1), (b1_col[:], b1),
                (qkv_bias[:, 0:1], bk),
                (qkv_bias[:, 1:2], bv),
                (qkv_bias[:, 2:QKV], bq),
                (exps_all[:], exps.partition_broadcast(P)), (bexps_all[:], bexps.partition_broadcast(P)),
                (gate[:], mask_weight.partition_broadcast(P)),
                (scales[:, 0:1], scale.partition_broadcast(P)), (scales[:, 1:2], biasscale.partition_broadcast(P)),
                (b_all[:], b.partition_broadcast(P)), (g2_all[:], g2.partition_broadcast(P)),
                (b2_all[:], b2.partition_broadcast(P)), (bo_all[:], bo.partition_broadcast(P)),
                (mask[:], causal), (cos[:], cos_t), (sin[:], sin_t),
            ]

            with nc.Block() as block:
                @block.sync
                def _(sp):
                    sp.dma_start(w_raw[:], W.rearrange("(k p) n -> p k n", p=P)).then_inc(w_in, 16)
                    for o in range(KH):
                        if o >= 2:
                            sp.wait_ge(wf_row, o - 1)
                        rows = slice(o * P, (o + 1) * P)
                        sp.dma_start(p_raw[:, o % 2, :], pweight[rows].rearrange("o i n -> o (i n)")).then_inc(f_in[o], 16)
                        sp.dma_start(n_raw[:, o % 2, :], nweight[rows].rearrange("o i n -> o (i n)")).then_inc(f_in[o], 16)

                @block.scalar
                def _(act):
                    for dst, src in small:
                        act.dma_start(dst, src).then_inc(small_in, 16)
                    act.dma_start(wqkv_raw[:, :, 0:P], Wk.rearrange("(k p) n -> p k n", p=P)).then_inc(wqkv_in, 16)
                    act.dma_start(wqkv_raw[:, :, P:2 * P], Wv.rearrange("(k p) n -> p k n", p=P)).then_inc(wqkv_in, 16)
                    act.dma_start(wqkv_raw[:, :, 2 * P:], Wq.rearrange("(k p) n -> p k n", p=P)).then_inc(wqkv_in, 16)
                    act.dma_start(wo_raw[:], Wo.rearrange("(k p) n -> p k n", p=P)).then_inc(wo_in, 16)
                    act.wait_ge(small_in, 16 * len(small))
                    nc.scalar.activation(gate[:], gate[:], ACT.Sigmoid).then_inc(gate_s, 1)
                    for o in range(KH):
                        act.wait_ge(f_in[o], 32)
                        nc.scalar.activation(p_raw[:, o % 2, :], p_raw[:, o % 2, :], ACT.Sigmoid).then_inc(f_gated, 1)
                        nc.scalar.activation(n_raw[:, o % 2, :], n_raw[:, o % 2, :], ACT.Sigmoid).then_inc(f_gated, 1)
                        if o == 0:
                            act.wait_ge(w_in, 16)
                            for k in range(KX):
                                nc.scalar.activation(w_hi[:, k, :], w_raw[:, k, :], ACT.Copy,
                                                     scale=g1_col[:, k:k + 1]).then_inc(w_hi_s, 1)
                        if o == 1:
                            act.wait_ge(wqkv_in, 48)
                            nc.scalar.activation(pairs(wqkv_hi), pairs(wqkv_raw), ACT.Copy).then_inc(wqkv_hi_s, 1)
                            act.wait_ge(wo_in, 16)
                            nc.scalar.activation(pairs(wo_hi), pairs(wo_raw), ACT.Copy).then_inc(wo_hi_s, 1)
                    act.wait_ge(wf_turned, KH)
                    for k in range(KH):
                        nc.scalar.activation(wf_hi[:, k, :], wf_bank[k][:], ACT.Copy).then_inc(wf_hi_s, 1)

                @block.gpsimd
                def _(pool):
                    nc.gpsimd.memset(ident[:], 0.0).then_inc(ident_step, 1)
                    nc.gpsimd.memset(minus_half[:], -0.5).then_inc(ident_step, 1)
                    pool.wait_ge(ident_step, 2)
                    nc.gpsimd.affine_select(out=ident[:], in_=ident[:], compare_op=ALU.not_equal, fill=1.0, base=0,
                                            pattern=[[-1, P]], channel_multiplier=1).then_inc(ident_step, 1)
                    pool.dma_start(pbias_all[:], pbias.rearrange("o n -> (o n)").partition_broadcast(P)).then_inc(bias_in, 16)
                    pool.dma_start(nbias_all[:], nbias.rearrange("o n -> (o n)").partition_broadcast(P)).then_inc(bias_in, 16)

                @block.tensor
                def _(pe):
                    pe.wait_ge(w_in, 16)
                    pe.wait_ge(b1_wide_s, 1)
                    for k in range(KX):
                        mm = nc.tensor.matmul(s_bank[0][:], b1_wide[:, k, :], w_raw[:, k, :],
                                              start=(k == 0), stop=(k == KX - 1))
                    mm.then_inc(y_const, 1)
                    pe.wait_ge(ident_step, 3)
                    for o in range(KH):
                        pe.wait_ge(wf_row, o + 1)
                        for k in range(KH):
                            mm = nc.tensor.transpose(wf_bank[k][:, o * P:(o + 1) * P],
                                                     wf_rows[:, o, k * P:(k + 1) * P], ident[:])
                        mm.then_inc(wf_turned, 1)

                @block.vector
                def _(dve):
                    steps = [0]

                    def after(ins):
                        steps[0] += 1
                        ins.then_inc(pre_dve, 1)
                        dve.wait_ge(pre_dve, steps[0])

                    dve.wait_ge(small_in, 16 * len(small))
                    nc.vector.tensor_copy(b1_wide[:], b1_col[:].unsqueeze(2).broadcast_to([P, KX, P])).then_inc(b1_wide_s, 1)
                    dve.wait_ge(gate_s, 1)
                    after(nc.vector.tensor_tensor(gate[:], gate[:], exps_all[:], ALU.mult))
                    after(nc.vector.tensor_scalar(gate[:], gate[:], scales[:, 0:1], None, ALU.mult))
                    for o in range(KH):
                        dve.wait_ge(f_gated, 2 * o + 2)
                        p = p_raw[:, o % 2, :]
                        after(nc.vector.tensor_tensor(p, p, n_raw[:, o % 2, :], ALU.subtract))
                        p3 = p.rearrange("p (i n) -> p i n", n=BITS)
                        after(nc.vector.tensor_tensor(p3, p3, gate[:].unsqueeze(1).broadcast_to([P, HID, BITS]), ALU.mult))
                        nc.vector.tensor_reduce(wf_rows[:, o, :], p3, AX_X, ALU.add).then_inc(wf_row, 1)
                        if o == 0:
                            for k in range(KX):
                                dve.wait_ge(w_hi_s, k + 1)
                                nc.vector.scalar_tensor_tensor(
                                    out=w_lo[:, k, :], in0=w_raw[:, k, :], scalar=g1_col[:, k:k + 1],
                                    in1=w_hi[:, k, :].bitcast(F32), op0=ALU.mult, op1=ALU.subtract)
                            dve.wait_ge(y_const, 1)
                            nc.vector.tensor_tensor(y_bias[:], s_bank[0][:], b_all[:], ALU.add)
                        if o == 1:
                            dve.wait_ge(wqkv_hi_s, 1)
                            nc.vector.tensor_tensor(pairs(wqkv_lo), pairs(wqkv_raw), pairs(wqkv_hi).bitcast(F32), ALU.subtract)
                            dve.wait_ge(wo_hi_s, 1)
                            nc.vector.tensor_tensor(pairs(wo_lo), pairs(wo_raw), pairs(wo_hi).bitcast(F32), ALU.subtract)
                    dve.wait_ge(bias_in, 32)
                    after(nc.vector.tensor_tensor(pbias_all[:], pbias_all[:], nbias_all[:], ALU.subtract))
                    d3 = pbias_all[:].rearrange("p (o n) -> p o n", n=BITS)
                    after(nc.vector.tensor_tensor(d3, d3, bexps_all[:].unsqueeze(1).broadcast_to([P, HID, BITS]), ALU.mult))
                    after(nc.vector.tensor_reduce(f_bias[:], d3, AX_X, ALU.add))
                    after(nc.vector.tensor_scalar(f_bias[:], f_bias[:], 1.0, -1.0, ALU.min, ALU.max))
                    after(nc.vector.tensor_scalar(f_bias[:], f_bias[:], STEP, ROUND, ALU.mult, ALU.add))
                    after(nc.vector.tensor_scalar(f_bias[:], f_bias[:], ROUND, 1.0 / STEP, ALU.subtract, ALU.mult))
                    after(nc.vector.tensor_scalar(f_bias[:], f_bias[:], scales[:, 1:2], None, ALU.mult))
                    for k in range(KH):
                        dve.wait_ge(wf_hi_s, k + 1)
                        nc.vector.tensor_tensor(wf_lo[:, k, :], wf_bank[k][:], wf_hi[:, k, :].bitcast(F32), ALU.subtract)

        x_tile = sb("x_tile", [P, 2, IN_DIM])
        act_hi, act_lo = sb("act_hi", [P, 3, HALF, P], F32R), sb("act_lo", [P, 3, HALF, P], F32R)
        h = sb("h", [P, 2, NT, HID])
        norm1, norm2 = sb("norm1", [P, HID]), sb("norm2", [P, HID])
        hT_hi, hT_lo = sb("hT_hi", [P, KH, TOK], F32R), sb("hT_lo", [P, KH, TOK], F32R)
        qk = sb("qk", [P, (1 + KH) * TOK + PAD + 1])
        shared = sb("shared", [P, 3 * HEADS * Q])
        swapped = shared[:, 0:KH * TOK]
        probT = shared[:, 0:2 * HEADS * Q].rearrange("p (c a q) -> p c a q", c=2, q=Q)
        oT = shared[:, 2 * HEADS * Q:].rearrange("p (g s q) -> p g s q", g=GROUPS, q=Q)
        vT = norm2[:].rearrange("p (s q) -> p s q", q=Q)
        k_diag = sb("k_diag", [P, GROUPS * PER * TOK + PAD + 1])
        v_diag = sb("v_diag", [P, CHUNKS, GROUPS, CHUNK, Q])
        prob = sb("prob", [P, 2, HEADS, Q])
        oT_hi, oT_lo = sb("oT_hi", [P, KH, TOK], F32R), sb("oT_lo", [P, KH, TOK], F32R)
        row_max, row_sum, row_inv = sb("row_max", [P, 2, HEADS]), sb("row_sum", [P, 2, HEADS]), sb("row_inv", [P, 2, HEADS])
        stats = sb("stats", [P, 2, 6])
        stats_of = {n: sb(f"stats_of_{n}", [P, 6]) for n in ("y", "h", "f")}
        mo = {n: sb(f"mo_{n}", [P, 5]) for n in ("x", "y", "h", "f")}

        def need(eng, s, count):
            if not isinstance(count, int) or count > 0:
                eng.wait_ge(s, count)

        def alone(eng):
            eng.sem_inc(waits_passed, 1)

        def wide(t, at, stride, n):
            a = t[:, at:at + 1]
            return bass.AP(a.tensor, a.offset, [list(a.ap[0]), [stride, n], [1, Q]])

        def table(t, n):
            return t[:].unsqueeze(1).broadcast_to([P, n, SEQ])

        def heads_of(t, c):
            return t[:, :, c * CTOK:(c + 1) * CTOK].rearrange("p g (s q) -> p g s q", q=SEQ)

        x_tokens = x.rearrange("b t f -> b (t f)")
        out_tokens = out.rearrange("b t d -> (b t) d")

        def run_steps(eng, step):
            step(0, True, False)
            step(1, True, True)
            with eng.Fori(0, (BATCHES - 2) // 2) as i:
                step(i * 2 + 2, True, True, 0)
                step(i * 2 + 3, True, True, 1)
            step(BATCHES, False, True)

        block = ctx.enter_context(nc.Block())

        @block.sync
        def _(sp):
            def step(s, embed, attend, parity=None):
                par = s % 2 if parity is None else parity
                for j in range(NT):
                    if embed:
                        need(sp, x_turned, 6 * s + 2 * j - 2)
                        alone(sp)
                        for row, seq, tok, n in pieces(j):
                            src = x_tokens[bass.ds(s * BATCH + seq, 1), tok * IN_DIM:(tok + n) * IN_DIM]
                            sp.dma_start(x_tile[row:row + n, (NT * par + j) % 2, :],
                                         src.rearrange("a (t d) -> (a t) d", d=IN_DIM)).then_inc(x_loaded[j], 16)
                    if attend and j == 1:
                        b = s - 1
                        sp.wait_ge(roped, len(ROPE) * b + 1)
                        alone(sp)
                        need(sp, s_acc, CHUNKS * b)
                        alone(sp)
                        for g in range(GROUPS):
                            for e in range(PER):
                                at = (g * PER + e) * TOK
                                sp.dma_start(k_diag[Q * e:Q * e + Q, at:at + TOK],
                                             qk[Q * g:Q * g + Q, 0:TOK]).then_inc(k_spread, 16)
            run_steps(sp, step)

        @block.tensor
        def _(pe):
            def x_turn(s, n):
                j, half = n // 2, n % 2
                par = (NT * parity_of[0] + j) % 2
                pe.wait_ge(x_normed, NT * s + j + 1)
                if n < 2:
                    need(pe, xT_lo_s, 6 * s)
                    need(pe, fT_lo_s, NT * (s - 1))
                else:
                    pe.wait_ge(xT_lo_s, 6 * s + n - 1)
                m = TILES[j][1]
                for k in range(HALF):
                    at = (half * HALF + k) * P
                    mm = nc.tensor.transpose(x_bank[half][:, k * P:k * P + m], x_tile[0:m, par, at:at + P], ident[0:m, 0:m])
                mm.then_inc(x_turned, 1)

            def split_product(bank, m, lhs, rhs, first, last, dep=None):
                (lh, ll), (rh, rl) = lhs, rhs
                nc.tensor.matmul(bank, lh, rh, start=first, stop=False)
                nc.tensor.matmul(bank, lh, rl, start=False, stop=False)
                return nc.tensor.matmul(bank, ll, rh, start=False, stop=last)

            def x_product(s, n):
                j, half, slot = n // 2, n % 2, n % 3
                m = TILES[j][1]
                pe.wait_ge(xT_lo_s, 6 * s + n + 1)
                if half == 0:
                    if j == 2:
                        pe.wait_ge(y_out, NT * s + 1)
                    else:
                        need(pe, qkv_out, QKV * (s - 1) + 5 + j)
                for k in range(HALF):
                    kk = half * HALF + k
                    mm = split_product(acc[j % 2][0:m, :], m, (act_hi[:, slot, k, 0:m], act_lo[:, slot, k, 0:m]),
                                       (w_hi[:, kk, :], w_lo[:, kk, :]), kk == 0, kk == KX - 1)
                mm.then_inc(x_used, 1)

            def h_turn(s, j):
                m = TILES[j][1]
                pe.wait_ge(h_normed, NT * s + j + 1)
                if j == 0:
                    need(pe, v_spread, CHUNK * s)
                else:
                    pe.wait_ge(hT_lo_s, NT * s + j)
                for k in range(KH):
                    mm = nc.tensor.transpose(turn_bank[:, k * P:k * P + m], norm1[0:m, k * P:(k + 1) * P], ident[0:m, 0:m])
                mm.then_inc(h_turned, 1)

            def qkv_block(b, n):
                if n == 0:
                    pe.wait_ge(hT_lo_s, NT * b + NT)
                    pe.wait_ge(y_out, NT * b + NT)
                elif n == 1:
                    pe.wait_ge(y_out, NT * b + NT - 1)
                else:
                    pe.wait_ge(qkv_out, QKV * b + n - 1)
                for k in range(KH):
                    cols = slice(n * P, (n + 1) * P)
                    mm = split_product(acc[n % 2][:, 0:TOK], P, (wqkv_hi[:, k, cols], wqkv_lo[:, k, cols]),
                                       (hT_hi[:, k, :], hT_lo[:, k, :]), k == 0, k == KH - 1)
                mm.then_inc(qkv_acc, 1)

            def v_turn(b):
                pe.wait_ge(qkv_out, QKV * b + 2)
                pe.wait_ge(hT_lo_s, NT * b + NT)
                for c in range(CHUNKS):
                    mm = nc.tensor.transpose(turn_bank[:, c * P:(c + 1) * P], 
                                             vT[:, c * CHUNK:(c + 1) * CHUNK, :].rearrange("p s q -> p (s q)"), ident[:])
                mm.then_inc(v_turned, 1)

            def scores(b, c):
                if c == 0:
                    pe.wait_ge(roped, len(ROPE) * b + 2)
                    pe.wait_ge(k_spread, 16 * GROUPS * PER * (b + 1))
                if c < 2:
                    need(pe, out_ready, NT * (b - 1) + 2 + c)
                else:
                    pe.wait_ge(s_masked, CHUNKS * b + c - 1)
                for g in range(GROUPS):
                    if c == 0 and g == 2:
                        pe.wait_ge(roped, len(ROPE) * b + 3)
                    for q in range(CHUNK):
                        tok = c * CTOK + q * SEQ
                        mm = nc.tensor.matmul(s_bank[c % 2][Q * q:Q * q + Q, g * P:(g + 1) * P],
                                              qk[:, (1 + g) * TOK + tok:(1 + g) * TOK + tok + Q],
                                              wide(k_diag, g * PER * TOK + tok, TOK, PER), start=True, stop=True)
                mm.then_inc(s_acc, 1)

            def values(b, c):
                pe.wait_ge(p_turned, CHUNKS * b + c + 1)
                if c == 0:
                    pe.wait_ge(v_spread, CHUNK * (b + 1))
                need(pe, o_turned, CHUNKS * b + c)
                for g in range(GROUPS):
                    mm = nc.tensor.matmul(o_bank[:, g * P:(g + 1) * P],
                                          probT[:, c % 2, g * PER:(g + 1) * PER, :].rearrange("p a q -> p (a q)"),
                                          v_diag[:, c, g, :, :].rearrange("p a d -> p (a d)"), start=True, stop=True)
                mm.then_inc(pv_acc, 1)

            def wo_tile(b, j):
                t, m = TILES[j]
                pe.wait_ge(oT_lo_s, CHUNKS * b + -(-(t + m) // CTOK))
                if j < 2:
                    pe.wait_ge(s_masked, CHUNKS * b + 3 + j)
                else:
                    pe.wait_ge(h2_ready, NT * b + 1)
                for k in range(KH):
                    mm = split_product(s_bank[j % 2][0:m, :], m, (oT_hi[:, k, t:t + m], oT_lo[:, k, t:t + m]),
                                       (wo_hi[:, k, :], wo_lo[:, k, :]), k == 0, k == KH - 1)
                mm.then_inc(wo_acc, 1)

            def f_turn(s, b, j, embed):
                m = TILES[j][1]
                pe.wait_ge(h2_normed, NT * b + j + 1)
                if j == 2:
                    pe.wait_ge(fT_lo_s, NT * b + 1)
                elif embed:
                    pe.wait_ge(xT_lo_s, 6 * s + 6)
                else:
                    pe.wait_ge(fT_lo_s, NT * b)
                for k in range(KH):
                    mm = nc.tensor.transpose(x_bank[j % 2][:, k * P:k * P + m], norm2[0:m, k * P:(k + 1) * P], ident[0:m, 0:m])
                mm.then_inc(f_turned, 1)

            def f_tile(b, j):
                m = TILES[j][1]
                pe.wait_ge(fT_lo_s, NT * b + j + 1)
                pe.wait_ge(*((h2_ready, NT * b + 2 + j) if j < 2 else (out_ready, NT * b + 1)))
                for k in range(KH):
                    mm = split_product(s_bank[1 - j % 2][0:m, :], m, (act_hi[:, j, k, 0:m], act_lo[:, j, k, 0:m]),
                                       (wf_hi[:, k, :], wf_lo[:, k, :]), k == 0, k == KH - 1)
                mm.then_inc(f_acc, 1)

            parity_of = [0]

            def step(s, embed, attend, parity=None):
                parity_of[0] = s % 2 if parity is None else parity
                b = s - 1
                if attend:
                    for n in range(4):
                        qkv_block(b, n)
                if embed:
                    x_turn(s, 0)
                if attend:
                    qkv_block(b, 4)
                if embed:
                    x_turn(s, 1)
                if attend:
                    qkv_block(b, 5)
                if embed:
                    x_turn(s, 2)
                    x_product(s, 0)
                    x_product(s, 1)
                if attend:
                    v_turn(b)
                    scores(b, 0)
                    scores(b, 1)
                if embed:
                    x_turn(s, 3)
                    x_product(s, 2)
                if attend:
                    scores(b, 2)
                if embed:
                    x_product(s, 3)
                if attend:
                    scores(b, 3)
                if embed:
                    h_turn(s, 0)
                if attend:
                    values(b, 0)
                if embed:
                    x_turn(s, 4)
                    x_turn(s, 5)
                if attend:
                    values(b, 1)
                if embed:
                    x_product(s, 4)
                if attend:
                    values(b, 2)
                    wo_tile(b, 0)
                if embed:
                    x_product(s, 5)
                if attend:
                    values(b, 3)
                    wo_tile(b, 1)
                    f_turn(s, b, 0, embed)
                if embed:
                    h_turn(s, 1)
                if attend:
                    wo_tile(b, 2)
                    f_turn(s, b, 1, embed)
                    f_tile(b, 0)
                if embed:
                    h_turn(s, 2)
                if attend:
                    f_turn(s, b, 2, embed)
                    f_tile(b, 1)
                    f_tile(b, 2)
            pe.wait_ge(zeroed, ZEROED)
            run_steps(pe, step)

        @block.scalar
        def _(act):
            def split_hi(dst, bank, m):
                return nc.scalar.activation(dst[:, :, 0:m], bank[:].rearrange("p (k t) -> p k t", k=HALF)[:, :, 0:m], ACT.Copy)

            def normalise(dst, src, m, key, ready, count, done):
                act.wait_ge(ready, count)
                nc.scalar.activation(dst, src, ACT.Identity, scale=mo[key][0:m, 3:4], bias=mo[key][0:m, 4:5]).then_inc(done, 1)

            def x_normalise(s, j, par):
                m = TILES[j][1]
                t = x_tile[0:m, (NT * par + j) % 2, :]
                normalise(t, t, m, "x", x_rstd, NT * s + j + 1, x_normed)

            def x_high(s, n):
                act.wait_ge(x_turned, 6 * s + n + 1)
                if n < 3:
                    need(act, f_acc, NT * (s - 2) + NT + n - 2)
                    need(act, x_used, 6 * s - 3 + n)
                else:
                    act.wait_ge(x_used, 6 * s + n - 2)
                split_hi(act_hi[:, n % 3], x_bank[n % 2], TILES[n // 2][1]).then_inc(xT_hi_s, 1)

            def qkv_evacuate(b, n):
                act.wait_ge(qkv_acc, QKV * b + n + 1)
                need(act, s_acc, CHUNKS * b)
                if n == 1:
                    dst = vT[:, :, 0:SEQ]
                    need(act, f_turned, NT * b)
                    need(act, v_turned, b)
                else:
                    at = max(n - 1, 0) * TOK
                    dst = qk[:, at:at + TOK]
                src = acc[n % 2][:, 0:TOK]
                if n == 1:
                    src = src.rearrange("p (s q) -> p s q", q=SEQ)
                nc.scalar.activation(dst, src, ACT.Identity, bias=qkv_bias[:, n:n + 1]).then_inc(qkv_out, 1)

            def spread_values(b):
                act.wait_ge(v_turned, b + 1)
                need(act, pv_acc, CHUNKS * b)
                for q in range(CHUNK):
                    rows = slice(Q * q, Q * q + Q)
                    nc.scalar.activation(v_diag[rows, :, :, q, :].rearrange("p c g d -> p (c g) d"),
                                         turn_bank[rows, :].rearrange("p (c d) -> p c d", d=Q), ACT.Copy).then_inc(v_spread, 1)

            def exponentials(b, c):
                act.wait_ge(s_shifted, CHUNKS * b + c + 1)
                nc.scalar.activation(prob[:, c % 2, :, 0:SEQ], prob[:, c % 2, :, 0:SEQ], ACT.Exp, scale=SCALE).then_inc(p_exp, 1)

            def h_normalise(s, j):
                m = TILES[j][1]
                need(act, h_turned, NT * s + j)
                normalise(norm1[0:m, :], h[0:m, par_now[0], j, :], m, "h", h_rstd, NT * s + j + 1, h_normed)

            def h_high(s, j):
                t, m = TILES[j]
                act.wait_ge(h_turned, NT * s + j + 1)
                need(act, qkv_acc, QKV * s)
                split_hi(hT_hi[:, :, t:t + m], turn_bank, m).then_inc(hT_hi_s, 1)

            def o_high(b, c):
                act.wait_ge(o_turned, CHUNKS * b + c + 1)
                need(act, wo_acc, NT * b)
                nc.scalar.activation(heads_of(oT_hi, c), oT[:, :, :, 0:SEQ], ACT.Copy).then_inc(oT_hi_s, 1)

            def f_normalise(b, j):
                m = TILES[j][1]
                need(act, f_turned, NT * b + j)
                act.wait_ge(v_turned, b + 1)
                normalise(norm2[0:m, :], h[0:m, 1 - par_now[0], j, :], m, "f", h2_rstd, NT * b + j + 1, h2_normed)

            def f_high(s, b, j, embed):
                act.wait_ge(f_turned, NT * b + j + 1)
                if embed:
                    act.wait_ge(x_used, 6 * s + 4 + j)
                else:
                    act.wait_ge(f_acc, NT * (b - 1) + j + 1)
                split_hi(act_hi[:, j], x_bank[j % 2], TILES[j][1]).then_inc(fT_hi_s, 1)

            def store(b, par):
                for j, (t, n) in enumerate(TILES):
                    act.wait_ge(out_ready, NT * b + j + 1)
                    alone(act)
                    act.dma_start(out_tokens[bass.ds(b * TOK + t, n), :], h[0:n, par, j, :]).then_inc(out_stored, 16)

            par_now = [0]

            def step(s, embed, attend, parity=None):
                par = par_now[0] = s % 2 if parity is None else parity
                b = s - 1
                if attend:
                    qkv_evacuate(b, 0)
                if embed:
                    x_normalise(s, 0, par)
                if not isinstance(s, int) or s >= 2:
                    store(s - 2, par)
                if attend:
                    qkv_evacuate(b, 1)
                    qkv_evacuate(b, 2)
                if embed:
                    x_normalise(s, 1, par)
                if attend:
                    qkv_evacuate(b, 3)
                if embed:
                    x_high(s, 0)
                if attend:
                    qkv_evacuate(b, 4)
                if embed:
                    x_high(s, 1)
                if attend:
                    qkv_evacuate(b, 5)
                if embed:
                    x_high(s, 2)
                if attend:
                    spread_values(b)
                    exponentials(b, 0)
                if embed:
                    x_high(s, 3)
                    h_normalise(s, 0)
                if attend:
                    exponentials(b, 1)
                if embed:
                    x_normalise(s, 2, par)
                if attend:
                    exponentials(b, 2)
                if embed:
                    h_high(s, 0)
                if attend:
                    o_high(b, 0)
                    exponentials(b, 3)
                if embed:
                    h_normalise(s, 1)
                if embed:
                    x_high(s, 4)
                    x_high(s, 5)
                if attend:
                    o_high(b, 1)
                    o_high(b, 2)
                    f_normalise(b, 0)
                    o_high(b, 3)
                if embed:
                    h_normalise(s, 2)
                if attend:
                    f_high(s, b, 0, embed)
                if embed:
                    h_high(s, 1)
                if attend:
                    f_normalise(b, 1)
                    f_high(s, b, 1, embed)
                    f_normalise(b, 2)
                if embed:
                    h_high(s, 2)
                if attend:
                    f_high(s, b, 2, embed)
            act.wait_ge(zeroed, ZEROED)
            run_steps(act, step)
            store(BATCHES - 1, (BATCHES - 1) % 2)
            act.wait_ge(out_stored, 16 * NT * BATCHES)

        @block.gpsimd
        def _(pool):
            def deviation(key, m, eps, moments, rstd, count):
                v = mo[key]
                pool.wait_ge(moments, count)
                alone(pool)
                nc.gpsimd.tensor_scalar(v[0:m, 2:3], v[0:m, 1:2], eps, None, ALU.add).then_inc(chain, 1)
                tick(1)
                last = key == "y"
                nc.gpsimd.tensor_tensor(v[0:m, 3:4], v[0:m, 2:3], minus_half[0:m, :], ALU.pow)\
                    .then_inc(rstd if last else chain, 1)
                if not last:
                    tick(1)
                    alone(pool)
                    nc.gpsimd.tensor_scalar(v[0:m, 4:5], v[0:m, 0:1], v[0:m, 3:4], -1.0, ALU.mult, ALU.mult).then_inc(rstd, 1)

            def tick(n):
                done[0] += n
                pool.wait_ge(chain, base[0] + done[0])

            def rope_cosine(b, n):
                first, blocks = ROPE[n]
                v = qk[:, first * TOK:(first + blocks) * TOK].rearrange("p (a t) -> p a t", t=SEQ)
                pool.wait_ge(rope_swapped, len(ROPE) * b + n + 1)
                nc.gpsimd.tensor_tensor(v, v, table(cos, blocks * BATCH), ALU.mult).then_inc(rope_cos, 1)

            def shift(b, c):
                v = prob[:, c % 2, :, 0:SEQ]
                pool.wait_ge(s_max, CHUNKS * b + c + 1)
                nc.gpsimd.tensor_tensor(v, v, row_max[:, c % 2, :].unsqueeze(2).broadcast_to([P, HEADS, SEQ]),
                                        ALU.subtract).then_inc(s_shifted, 1)

            def divide(b, c):
                v = prob[:, c % 2, :, 0:SEQ]
                pool.wait_ge(p_inv, CHUNKS * b + c + 1)
                nc.gpsimd.tensor_tensor(v, v, row_inv[:, c % 2, :].unsqueeze(2).broadcast_to([P, HEADS, SEQ]),
                                        ALU.mult).then_inc(p_scaled, 1)

            def add_output_bias(b, j):
                m = TILES[j][1]
                t = h[0:m, 1 - par_now[0], j, :]
                pool.wait_ge(h_normed, NT * b + j + 1)
                nc.gpsimd.tensor_tensor(t, t, bo_all[0:m, :], ALU.add).then_inc(h_biased, 1)

            def add_ffn_bias(b, j):
                m = TILES[j][1]
                t = h[0:m, 1 - par_now[0], j, :]
                pool.wait_ge(h2_normed, NT * b + j + 1)
                nc.gpsimd.tensor_tensor(t, t, f_bias[0:m, :], ALU.add).then_inc(out_biased, 1)

            par_now, done, base = [0], [0], [0]
            EMBED_STEPS, ATTEND_STEPS = NT * (2 + 1 + 2), NT * 2

            def step(s, embed, attend, parity=None):
                par_now[0] = s % 2 if parity is None else parity
                b = s - 1
                done[0] = 0
                base[0] = EMBED_STEPS * s + (ATTEND_STEPS * b if attend else 0)

                def x_dev(j):
                    deviation("x", TILES[j][1], EPS_TOK, x_moments, x_rstd, NT * s + j + 1)

                def y_dev(j):
                    deviation("y", TILES[j][1], EPS_TOK, y_moments, y_rstd, NT * s + j + 1)

                def h_dev(j):
                    deviation("h", TILES[j][1], EPS_LN, h_moments, h_rstd, NT * s + j + 1)

                def f_dev(j):
                    deviation("f", TILES[j][1], EPS_LN, h2_moments, h2_rstd, NT * b + j + 1)

                if embed:
                    x_dev(0)
                if attend:
                    rope_cosine(b, 0)
                if embed:
                    x_dev(1)
                if attend:
                    rope_cosine(b, 1)
                    rope_cosine(b, 2)
                    for j in range(NT):
                        add_output_bias(b, j)
                if embed:
                    y_dev(0)
                if attend:
                    shift(b, 0)
                if embed:
                    h_dev(0)
                if attend:
                    shift(b, 1)
                    divide(b, 0)
                if embed:
                    x_dev(2)
                if attend:
                    divide(b, 1)
                    shift(b, 2)
                if embed:
                    y_dev(1)
                if attend:
                    divide(b, 2)
                    shift(b, 3)
                if embed:
                    h_dev(1)
                if attend:
                    divide(b, 3)
                    f_dev(0)
                if embed:
                    y_dev(2)
                    h_dev(2)
                if attend:
                    f_dev(1)
                    add_ffn_bias(b, 0)
                    f_dev(2)
                    add_ffn_bias(b, 1)
                    add_ffn_bias(b, 2)
            for ap in (qk[:, (1 + KH) * TOK:], norm2[:], k_diag[:], v_diag[:], prob[:]):
                nc.gpsimd.memset(ap, 0.0).then_inc(zeroed, 1)
            pool.wait_ge(zeroed, ZEROED)
            run_steps(pool, step)

        @block.vector
        def _(dve):
            def moments(key, src, m, done, count):
                n = src.shape[-1] // 512
                for i in range(n):
                    ins = nc.vector.bn_stats(stats[0:m, 0 if key != "x" else i, :] if key == "x" else stats_of[key][0:m, :],
                                             src[:, i * 512:(i + 1) * 512]).then_inc(st[key], 1)
                dve.wait_ge(st[key], count * n)
                src6 = stats[0:m, 0:2, :].rearrange("p a b -> p (a b)") if key == "x" else stats_of[key][0:m, :]
                alone(dve)
                nc.vector.bn_aggr(mo[key][0:m, 0:2], src6).then_inc(done, 1)

            def x_stats(s, j, par):
                m = TILES[j][1]
                dve.wait_ge(x_loaded[j], 16 * len(pieces(j)) * (s + 1))
                need(dve, x_normed, NT * s + j)
                moments("x", x_tile[0:m, (NT * par + j) % 2, :], m, x_moments, NT * s + j + 1)

            def split_lo(dst, bank, hi, m):
                return nc.vector.tensor_tensor(dst[:, :, 0:m], bank[:].rearrange("p (k t) -> p k t", k=HALF)[:, :, 0:m],
                                               hi[:, :, 0:m].bitcast(F32), ALU.subtract)

            def x_low(s, n):
                dve.wait_ge(xT_hi_s, 6 * s + n + 1)
                split_lo(act_lo[:, n % 3], x_bank[n % 2], act_hi[:, n % 3], TILES[n // 2][1]).then_inc(xT_lo_s, 1)

            def rope_part(b, n):
                first, blocks = ROPE[n]
                at = max(first - 1, 0) * TOK
                return qk[:, first * TOK:(first + blocks) * TOK], swapped[:, at:at + blocks * TOK], blocks

            def rope_sine(b, n):
                v, w, blocks = rope_part(b, n)
                dve.wait_ge(qkv_out, QKV * b + (1 if n == 0 else 2 * n + 2))
                if n == 0:
                    need(dve, pv_acc, CHUNKS * b)
                    need(dve, oT_lo_s, CHUNKS * b)
                if n == 1:
                    dve.wait_ge(roped, len(ROPE) * b + 1)
                alone(dve)
                nc.vector.stream_shuffle(w, v, [(i + HEAD // 2) % Q for i in range(Q)]).then_inc(rope_swapped, 1)
                dve.wait_ge(rope_swapped, len(ROPE) * b + n + 1)
                w3 = w.rearrange("p (a t) -> p a t", t=SEQ)
                nc.vector.tensor_tensor(w3, w3, table(sin, blocks * BATCH), ALU.mult).then_inc(rope_sin, 1)

            def rope_sum(b, n):
                v, w, blocks = rope_part(b, n)
                dve.wait_ge(rope_sin, len(ROPE) * b + n + 1)
                dve.wait_ge(rope_cos, len(ROPE) * b + n + 1)
                nc.vector.tensor_tensor(v, v, w, ALU.add).then_inc(roped, 1)

            def y_evacuate(s, j):
                m = TILES[j][1]
                t = h[0:m, par_now[0], j, :]
                dve.wait_ge(x_used, 6 * s + 2 * j + 2)
                need(dve, out_stored, 16 * (NT * (s - 2) + NT))
                nc.vector.tensor_tensor(t, acc[j % 2][0:m, :], y_bias[0:m, :], ALU.add).then_inc(y_out, 1)
                dve.wait_ge(y_out, NT * s + j + 1)
                need(dve, h_ready, NT * s + j)
                moments("y", t, m, y_moments, NT * s + j + 1)

            def y_centre(s, j):
                m = TILES[j][1]
                t = h[0:m, par_now[0], j, :]
                dve.wait_ge(y_moments, NT * s + j + 1)
                nc.vector.scalar_tensor_tensor(out=t, in0=t, scalar=mo["y"][0:m, 0:1], in1=g2_all[0:m, :],
                                               op0=ALU.subtract, op1=ALU.mult).then_inc(h_gained, 1)

            def y_scale(s, j):
                m = TILES[j][1]
                t = h[0:m, par_now[0], j, :]
                dve.wait_ge(y_rstd, NT * s + j + 1)
                dve.wait_ge(h_gained, NT * s + j + 1)
                nc.vector.scalar_tensor_tensor(out=t, in0=t, scalar=mo["y"][0:m, 3:4], in1=b2_all[0:m, :],
                                               op0=ALU.mult, op1=ALU.add).then_inc(h_ready, 1)

            def mask_scores(b, c):
                v = prob[:, c % 2, :, 0:SEQ]
                dve.wait_ge(s_acc, CHUNKS * b + c + 1)
                need(dve, p_turned, CHUNKS * b + c - 1)
                nc.vector.tensor_tensor(v, s_bank[c % 2][:].rearrange("p (a k) -> p a k", k=Q)[:, :, 0:SEQ],
                                        mask[:].unsqueeze(1).broadcast_to([P, HEADS, SEQ]), ALU.add).then_inc(s_masked, 1)
                dve.wait_ge(s_masked, CHUNKS * b + c + 1)
                nc.vector.tensor_reduce(row_max[:, c % 2, :], v, AX_X, ALU.max).then_inc(s_max, 1)

            def sum_up(b, c):
                dve.wait_ge(p_exp, CHUNKS * b + c + 1)
                need(dve, p_scaled, CHUNKS * b + c - 1)
                nc.vector.tensor_reduce(row_sum[:, c % 2, :], prob[:, c % 2, :, 0:SEQ], AX_X, ALU.add).then_inc(p_sum, 1)
                dve.wait_ge(p_sum, CHUNKS * b + c + 1)
                nc.vector.reciprocal(row_inv[:, c % 2, :], row_sum[:, c % 2, :]).then_inc(p_inv, 1)

            def turn_probs(b, c):
                dve.wait_ge(p_scaled, CHUNKS * b + c + 1)
                need(dve, pv_acc, CHUNKS * b + c - 1)
                if c == 0:
                    dve.wait_ge(roped, len(ROPE) * (b + 1))
                nc.vector.transpose(probT[:, c % 2].rearrange("p a q -> p (a q)"),
                                    prob[:, c % 2].rearrange("p a q -> p (a q)")).then_inc(p_turned, 1)

            def turn_heads(b, c):
                dve.wait_ge(pv_acc, CHUNKS * b + c + 1)
                need(dve, oT_hi_s, CHUNKS * b + c)
                need(dve, oT_lo_s, CHUNKS * b + c)
                nc.vector.transpose(oT.rearrange("p g s q -> p (g s q)"), o_bank[:]).then_inc(o_turned, 1)

            def o_low(b, c):
                dve.wait_ge(oT_hi_s, CHUNKS * b + c + 1)
                nc.vector.tensor_tensor(heads_of(oT_lo, c), oT[:, :, :, 0:SEQ],
                                        heads_of(oT_hi, c).bitcast(F32), ALU.subtract).then_inc(oT_lo_s, 1)

            def h_stats(s, j):
                m = TILES[j][1]
                dve.wait_ge(h_ready, NT * s + j + 1)
                need(dve, h_normed, NT * s + j)
                moments("h", h[0:m, par_now[0], j, :], m, h_moments, NT * s + j + 1)

            def h_low(s, j):
                t, m = TILES[j]
                dve.wait_ge(hT_hi_s, NT * s + j + 1)
                split_lo(hT_lo[:, :, t:t + m], turn_bank, hT_hi[:, :, t:t + m], m).then_inc(hT_lo_s, 1)

            def add_attention(b, j):
                m = TILES[j][1]
                t = h[0:m, 1 - par_now[0], j, :]
                dve.wait_ge(wo_acc, NT * b + j + 1)
                dve.wait_ge(h_biased, NT * b + j + 1)
                nc.vector.tensor_tensor(t, s_bank[j % 2][0:m, :], t, ALU.add).then_inc(h2_ready, 1)
                dve.wait_ge(h2_ready, NT * b + j + 1)
                need(dve, h2_normed, NT * b + j)
                moments("f", t, m, h2_moments, NT * b + j + 1)

            def f_low(b, j):
                dve.wait_ge(fT_hi_s, NT * b + j + 1)
                split_lo(act_lo[:, j], x_bank[j % 2], act_hi[:, j], TILES[j][1]).then_inc(fT_lo_s, 1)

            def add_ffn(b, j):
                m = TILES[j][1]
                t = h[0:m, 1 - par_now[0], j, :]
                dve.wait_ge(f_acc, NT * b + j + 1)
                dve.wait_ge(out_biased, NT * b + j + 1)
                nc.vector.tensor_tensor(t, s_bank[1 - j % 2][0:m, :], t, ALU.add).then_inc(out_ready, 1)

            par_now = [0]

            def step(s, embed, attend, parity=None):
                par = par_now[0] = s % 2 if parity is None else parity
                b = s - 1
                if embed:
                    x_stats(s, 0, par)
                if attend:
                    rope_sine(b, 0)
                if embed:
                    x_stats(s, 1, par)
                if attend:
                    rope_sum(b, 0)
                    rope_sine(b, 1)
                if embed:
                    x_low(s, 0)
                if attend:
                    rope_sum(b, 1)
                if embed:
                    x_low(s, 1)
                if attend:
                    rope_sine(b, 2)
                if embed:
                    x_low(s, 2)
                if attend:
                    rope_sum(b, 2)
                if embed:
                    y_evacuate(s, 0)
                    y_centre(s, 0)
                if attend:
                    mask_scores(b, 0)
                if embed:
                    y_scale(s, 0)
                    h_stats(s, 0)
                if attend:
                    mask_scores(b, 1)
                if embed:
                    x_low(s, 3)
                if attend:
                    sum_up(b, 0)
                if embed:
                    x_stats(s, 2, par)
                if attend:
                    sum_up(b, 1)
                    turn_probs(b, 0)
                    mask_scores(b, 2)
                    turn_probs(b, 1)
                    turn_heads(b, 0)
                if embed:
                    y_evacuate(s, 1)
                    y_centre(s, 1)
                if attend:
                    sum_up(b, 2)
                    mask_scores(b, 3)
                if embed:
                    y_scale(s, 1)
                    h_stats(s, 1)
                    h_low(s, 0)
                if attend:
                    turn_probs(b, 2)
                    o_low(b, 0)
                    sum_up(b, 3)
                if embed:
                    x_low(s, 4)
                    x_low(s, 5)
                if attend:
                    turn_heads(b, 1)
                    o_low(b, 1)
                    turn_probs(b, 3)
                    turn_heads(b, 2)
                    o_low(b, 2)
                    add_attention(b, 0)
                if embed:
                    y_evacuate(s, 2)
                    y_centre(s, 2)
                if attend:
                    turn_heads(b, 3)
                    o_low(b, 3)
                if embed:
                    y_scale(s, 2)
                    h_stats(s, 2)
                if attend:
                    add_attention(b, 1)
                    f_low(b, 0)
                if embed:
                    h_low(s, 1)
                if attend:
                    add_attention(b, 2)
                    f_low(b, 1)
                    add_ffn(b, 0)
                if embed:
                    h_low(s, 2)
                if attend:
                    f_low(b, 2)
                    add_ffn(b, 1)
                    add_ffn(b, 2)
            dve.wait_ge(zeroed, ZEROED)
            run_steps(dve, step)


_INS = ["x", "L0_tok_W", "L0_tok_b", "L0_tok_g1", "L0_tok_b1", "L0_tok_g2", "L0_tok_b2", "L0_attn_Wq", "L0_attn_bq",
        "L0_attn_Wk", "L0_attn_bk", "L0_attn_Wv", "L0_attn_bv", "L0_attn_Wo", "L0_attn_bo", "L0_ffn_pweight",
        "L0_ffn_nweight", "L0_ffn_exps", "L0_ffn_bexps", "L0_ffn_mask_weight", "L0_ffn_scale", "L0_ffn_pbias",
        "L0_ffn_nbias", "L0_ffn_biasscale"]


def shape_tables():
    inv = 1.0 / 10000.0 ** (np.arange(HEAD // 2, dtype=np.float32) * 2.0 / HEAD)
    angle = inv.astype(np.float32)[:, None] * np.arange(SEQ, dtype=np.float32)[None, :]
    cos, sin = np.cos(angle), np.sin(angle)
    cos = np.tile(np.concatenate([cos, cos]), (P // Q, 1)).astype(np.float32)
    sin = np.tile(np.concatenate([-sin, sin]), (P // Q, 1)).astype(np.float32)
    query, key = np.arange(Q)[:, None], np.arange(SEQ)[None, :]
    causal = np.tile(np.where(key <= query, 0.0, NEG), (P // Q, 1)).astype(np.float32)
    return {"cos": cos, "sin": sin, "causal": causal}


def kernel(**inputs):
    import concourse.bacc as _bacc
    from concourse.bass_utils import run_bass_kernel_spmd as _run

    nc = _bacc.Bacc("TRN2", target_bir_lowering=False, num_devices=1)
    arrays, args = {}, []
    given = {name: np.asarray(inputs[name]) for name in _INS} | shape_tables()
    for name in ("L0_tok_g1", "L0_tok_b1", "L0_attn_bq", "L0_attn_bk", "L0_attn_bv"):
        given[name] = given[name].reshape(-1, P).T
    given = {name: np.ascontiguousarray(a) for name, a in given.items()}
    for name, a in given.items():
        arrays[f"in_{name}_dram"] = a
        args.append(nc.dram_tensor(f"in_{name}_dram", a.shape, mybir.dt.from_np(a.dtype), kind="ExternalInput").ap())
    args.append(nc.dram_tensor("out_0_dram", (SEQS, SEQ, HID), F32, kind="ExternalOutput").ap())
    audio_tower(nc, *args)
    r = _run(nc, [arrays], core_ids=[0])
    return r.results[0]["out_0_dram"]
```

```python
from contextlib import ExitStack

import numpy as np
import concourse.bass as bass
from concourse import mybir

ALU = mybir.AluOpType
ACT = mybir.ActivationFunctionType
AX_X = mybir.AxisListType.X
F32 = mybir.dt.float32
F32R = mybir.dt.float32r

P = 128
Q = 32
SEQS, FRAMES, FEAT = 128, 375, 64
TIN = 16
IN_DIM = TIN * FEAT
HID = 512
HEADS, GROUPS, HEAD = 16, 4, 32
PER = HEADS // GROUPS
BITS = 4
SEQ = FRAMES // TIN
BATCH = 16
BATCHES = SEQS // BATCH
TOK = BATCH * SEQ
TILES = [(t, min(P, TOK - t)) for t in range(0, TOK, P)]
NT = len(TILES)
CHUNK = 4
CHUNKS = BATCH // CHUNK
CTOK = CHUNK * SEQ
KX = IN_DIM // P
KH = HID // P
HALF = 4
QKV = 2 + KH
ROPE = [(0, 1), (1, 2), (3, 2)]
PAD = Q - SEQ
EPS_TOK, EPS_LN = 1e-6, 1e-5
STEP = float(2 ** BITS - 1)
NEG = -3.0e38
UNITS = 2 * KH
UNIT = HID // 2 * BITS
ROWS = ["L0_tok_b", "L0_tok_g2", "L0_tok_b2", "L0_attn_bo"]
COLUMNS = 2 * KX + 2 * KH * BITS
GATES = 3 * BITS + 2
CONSTS = 4
QK_ZERO, V_ZERO, PROB_ZERO, K_ZERO = 1, 2, 3, 5
ROUND = 1.5 * 2.0 ** 23
SCALE = HEAD ** -0.5


def pieces(j):
    at, end, out = TILES[j][0], TILES[j][0] + TILES[j][1], []
    while at < end:
        whole = (end - at) // SEQ if at % SEQ == 0 else 0
        n = SEQ if whole else min(SEQ - at % SEQ, end - at)
        out.append((at - TILES[j][0], at // SEQ, at % SEQ, max(whole, 1), n))
        at += max(whole, 1) * n
    return out


def audio_tower(nc, x, W, Wqkv, Wo, pweight, nweight, rows_in, gates_in, columns_in, qkv_bias_in, tables_in, out):
    with ExitStack() as ctx:
        def sb(name, shape, dt=F32):
            return ctx.enter_context(nc.sbuf_tensor(name, shape, dt))

        def pb(name):
            return ctx.enter_context(nc.psum_tensor(name, [P, 512], F32))

        def sem(name):
            return ctx.enter_context(nc.semaphore(name))

        w_hi, w_lo = sb("w_hi", [P, KX, HID], F32R), sb("w_lo", [P, KX, HID], F32R)
        wqkv_hi, wqkv_lo = sb("wqkv_hi", [P, KH, QKV * P], F32R), sb("wqkv_lo", [P, KH, QKV * P], F32R)
        wo_hi, wo_lo = sb("wo_hi", [P, KH, HID], F32R), sb("wo_lo", [P, KH, HID], F32R)
        wf_hi, wf_lo = sb("wf_hi", [P, KH, HID], F32R), sb("wf_lo", [P, KH, HID], F32R)
        rows_all = sb("rows_all", [P, len(ROWS), HID])
        y_bias, g2_all, b2_all, bo_all = (rows_all[:, i, :] for i in range(len(ROWS)))
        f_bias = sb("f_bias", [P, HID])
        tables = sb("tables", [P, 3, SEQ])
        cos, sin, mask = (tables[:, i, :] for i in range(3))
        ident = sb("ident", [P, P])
        qkv_bias = sb("qkv_bias", [P, QKV])
        minus_half = sb("minus_half", [P, 1])
        x_bank = [pb("x_bank0"), pb("x_bank1")]
        turn_bank = pb("turn_bank")
        acc = [pb("acc0"), pb("acc1")]
        s_bank = [pb("s_bank0"), pb("s_bank1")]
        o_bank = pb("o_bank")

        x_loaded = [sem(f"x_loaded{j}") for j in range(NT)]
        (x_moments, x_rstd, x_normed, x_turned, xT_hi_s, xT_lo_s, x_used) = map(sem, (
            "x_moments", "x_rstd", "x_normed", "x_turned", "xT_hi", "xT_lo", "x_used"))
        (y_out, y_moments, y_rstd, h_gained, h_ready) = map(sem, (
            "y_out", "y_moments", "y_rstd", "h_gained", "h_ready"))
        (h_moments, h_rstd, h_normed, h_turned, hT_hi_s, hT_lo_s) = map(sem, (
            "h_moments", "h_rstd", "h_normed", "h_turned", "hT_hi_s", "hT_lo_s"))
        (qkv_acc, qkv_out, rope_swapped, rope_cos, rope_sin, roped, k_spread) = map(sem, (
            "qkv_acc", "qkv_out", "rope_swapped", "rope_cos", "rope_sin", "roped", "k_spread"))
        (v_turned, v_spread, s_acc, s_masked, s_max, s_shifted, p_exp, p_sum, p_inv, p_scaled, p_turned) = map(sem, (
            "v_turned", "v_spread", "s_acc", "s_masked", "s_max", "s_shifted", "p_exp", "p_sum", "p_inv",
            "p_scaled", "p_turned"))
        (pv_acc, o_turned, oT_hi_s, oT_lo_s, wo_acc, h_biased, h2_ready, h2_moments, h2_rstd, h2_normed) = map(sem, (
            "pv_acc", "o_turned", "oT_hi_s", "oT_lo_s", "wo_acc", "h_biased", "h2_ready", "h2_moments",
            "h2_rstd", "h2_normed"))
        (f_turned, fT_hi_s, fT_lo_s, f_acc, out_biased, out_ready, out_stored) = map(sem, (
            "f_turned", "fT_hi_s", "fT_lo_s", "f_acc", "out_biased", "out_ready", "out_stored"))
        st = {n: sem(f"stats_{n}") for n in ("x", "y", "h", "f")}
        zeroed, chain, waits_passed = sem("zeroed"), sem("chain"), sem("waits_passed")
        (rows_here, gates_here, columns_here, qkv_bias_here, tables_here, wo_here) = map(sem, (
            "rows_here", "gates_here", "columns_here", "qkv_bias_here", "tables_here", "wo_here"))
        w_here = [sem(f"w_here{i}") for i in range(KX // 2)]
        wqkv_here = [sem(f"wqkv_here{i}") for i in range(2)]
        unit_here = [sem(f"unit_here{i}") for i in range(4)]
        (const_step, gate_sig, gate_step, gate_ready, f_step, f_diag_ready) = map(sem, (
            "const_step", "gate_sig", "gate_step", "gate_ready", "f_step", "f_diag_ready"))
        (b1_wide_ready, y_const, y_bias_ready, f_bias_acc, f_bias_ready) = map(sem, (
            "b1_wide_ready", "y_const", "y_bias_ready", "f_bias_acc", "f_bias_ready"))
        (w_hi_s, w_lo_s, wqkv_hi_s, wqkv_lo_s, wo_hi_s, wo_lo_s, wf_hi_s, wf_lo_s) = map(sem, (
            "w_hi_s", "w_lo_s", "wqkv_hi_s", "wqkv_lo_s", "wo_hi_s", "wo_lo_s", "wf_hi_s", "wf_lo_s"))
        unit_gated, unit_diff, unit_diff_dve, unit_used = map(sem, ("unit_gated", "unit_diff", "unit_diff_dve", "unit_used"))

        x_tile = sb("x_tile", [P, 2, IN_DIM])
        act_hi, act_lo = sb("act_hi", [P, 3, HALF, P], F32R), sb("act_lo", [P, 3, HALF, P], F32R)
        h = sb("h", [P, 2, NT, HID])
        norm = sb("norm", [P, 2, HID])
        norm1, norm2 = norm[:, 0, :], norm[:, 1, :]
        hT_hi, hT_lo = sb("hT_hi", [P, KH, TOK], F32R), sb("hT_lo", [P, KH, TOK], F32R)
        qk = sb("qk", [P, (1 + KH) * TOK + PAD + 1])
        shared = sb("shared", [P, 3 * HEADS * Q])
        swapped = shared[:, 0:KH * TOK]
        probT = shared[:, 0:2 * HEADS * Q].rearrange("p (c a q) -> p c a q", c=2, q=Q)
        oT = shared[:, 2 * HEADS * Q:].rearrange("p (g s q) -> p g s q", g=GROUPS, q=Q)
        vT = norm2.rearrange("p (s q) -> p s q", q=Q)
        k_diag = sb("k_diag", [P, GROUPS * PER * TOK + PAD + 1])
        v_diag = sb("v_diag", [P, CHUNKS, GROUPS, CHUNK, Q])
        prob = sb("prob", [P, 2, HEADS, Q])
        oT_hi, oT_lo = sb("oT_hi", [P, KH, TOK], F32R), sb("oT_lo", [P, KH, TOK], F32R)
        row_max, row_sum, row_inv = sb("row_max", [P, 2, HEADS]), sb("row_sum", [P, 2, HEADS]), sb("row_inv", [P, 2, HEADS])
        stats = sb("stats", [P, 2, 6])
        stats_of = {n: sb(f"stats_of_{n}", [P, 6]) for n in ("y", "h", "f")}
        mo = {n: sb(f"mo_{n}", [P, 5]) for n in ("x", "y", "h", "f")}

        W_LEN = KX * HID
        w_raw = k_diag[:, 0:W_LEN].rearrange("p (k n) -> p k n", n=HID)
        wqkv_raw = [a.rearrange("p (k n) -> p k n", n=QKV * P)
                    for a in (h[:, 1].rearrange("p j n -> p (j n)"), shared[:, 0:NT * HID])]
        wo_raw = v_diag[:].rearrange("p c g a d -> p (c g a d)").rearrange("p (k n) -> p k n", n=HID)
        b1_wide = norm[:].rearrange("p a n -> p (a n)").rearrange("p (k q) -> p k q", q=P)
        prob_flat = prob[:].rearrange("p c a q -> p (c a q)")
        unit_p = [qk[:, 0:UNIT], k_diag[:, 0:UNIT], k_diag[:, 2 * UNIT:3 * UNIT], h[:, 1].rearrange("p j n -> p (j n)")[:, 0:UNIT]]
        unit_n = [prob_flat, k_diag[:, UNIT:2 * UNIT], k_diag[:, 3 * UNIT:4 * UNIT], shared[:, 0:UNIT]]
        taken = [W_LEN]

        def spare(n):
            taken[0] += n
            return k_diag[:, taken[0] - n:taken[0]]

        ones, gate_diag, f_diag = spare(P), spare(BITS * P).rearrange("p (n q) -> p n q", q=P), spare(KH * P).rearrange("p (k q) -> p k q", q=P)
        columns = spare(COLUMNS)
        g1_col, b1_col = columns[:, 0:KX], columns[:, KX:2 * KX]
        pbias, nbias = (columns[:, 2 * KX + i * KH * BITS:2 * KX + (i + 1) * KH * BITS] for i in range(2))
        gates = spare(GATES)
        exps, bexps, gate = (gates[:, i * BITS:(i + 1) * BITS] for i in range(3))
        scale, biasscale = gates[:, 3 * BITS:3 * BITS + 1], gates[:, 3 * BITS + 1:3 * BITS + 2]
        f_col = spare(KH)

        def y_bank(s, j):
            return s_bank[0] if j == 0 and not first(s) else acc[j % 2]

        def first(b):
            return isinstance(b, int) and b == 0

        def need(eng, s, count):
            if not isinstance(count, int) or count > 0:
                eng.wait_ge(s, count)

        def alone(eng):
            eng.sem_inc(waits_passed, 1)

        def wide(t, at, stride, n):
            a = t[:, at:at + 1]
            return bass.AP(a.tensor, a.offset, [list(a.ap[0]), [stride, n], [1, Q]])

        def table(t, n):
            return t.unsqueeze(1).broadcast_to([P, n, SEQ])

        def heads_of(t, c):
            return t[:, :, c * CTOK:(c + 1) * CTOK].rearrange("p g (s q) -> p g s q", q=SEQ)

        x_tokens = x.rearrange("b t f -> b (t f)")
        out_tokens = out.rearrange("b t d -> (b t) d")

        def run_steps(eng, step, last_step):
            step(1, True, True)
            with eng.Fori(0, (BATCHES - 2) // 2) as i:
                step(i * 2 + 2, True, True, 0)
                step(i * 2 + 3, True, True, 1)
            last_step()

        block = ctx.enter_context(nc.Block())

        @block.sync
        def _(sp):
            def load_x(s, j, par):
                need(sp, x_turned, 6 * s + 2 * j - 2)
                alone(sp)
                for row, seq, tok, seqs, n in pieces(j):
                    src = x_tokens[bass.ds(s * BATCH + seq, seqs), tok * IN_DIM:(tok + n) * IN_DIM]
                    sp.dma_start(x_tile[row:row + seqs * n, (NT * par + j) % 2, :],
                                 src.rearrange("a (t d) -> a t d", d=IN_DIM)).then_inc(x_loaded[j], 16)

            def store(b, par):
                for j, (t, n) in enumerate(TILES):
                    sp.wait_ge(out_ready, NT * b + j + 1)
                    alone(sp)
                    sp.dma_start(out_tokens[bass.ds(b * TOK + t, n), :], h[0:n, par, j, :]).then_inc(out_stored, 16)

            def load_unit(u):
                rows, inputs = slice(u // 2 * P, (u // 2 + 1) * P), slice(u % 2 * (HID // 2), (u % 2 + 1) * (HID // 2))
                sp.dma_start(unit_p[u % 4], pweight[rows, inputs].rearrange("o i n -> o (i n)")).then_inc(unit_here[u % 4], 16)
                sp.dma_start(unit_n[u % 4], nweight[rows, inputs].rearrange("o i n -> o (i n)")).then_inc(unit_here[u % 4], 16)

            def load_w(i):
                sp.dma_start(w_raw[:, 2 * i:2 * i + 2, :],
                             W[2 * i * P:(2 * i + 2) * P].rearrange("(k p) n -> p k n", p=P)).then_inc(w_here[i], 16)

            def first_step():
                load_x(0, 0, 0)
                load_w(0)
                load_w(1)
                load_x(0, 1, 0)
                load_w(2)
                load_w(3)
                for i in range(2):
                    sp.dma_start(wqkv_raw[i], Wqkv[i * 2 * P:(i + 1) * 2 * P].rearrange("(k p) n -> p k n", p=P)).then_inc(wqkv_here[i], 16)
                load_unit(0)
                load_x(0, 2, 0)
                sp.dma_start(wo_raw, Wo.rearrange("(k p) n -> p k n", p=P)).then_inc(wo_here, 16)
                sp.wait_ge(y_const, 1)
                sp.wait_ge(w_lo_s, KX // 2)
                load_unit(1)
                sp.wait_ge(w_lo_s, KX)
                load_unit(2)
                sp.wait_ge(wqkv_lo_s, 2)
                load_unit(3)
                for u in range(4, UNITS):
                    sp.wait_ge(unit_used, u - 3)
                    load_unit(u)

            def step(s, embed, attend, parity=None):
                par = s % 2 if parity is None else parity
                if embed:
                    load_x(s, 0, par)
                    load_x(s, 1, par)
                if not isinstance(s, int) or s >= 2:
                    store(s - 2, par)
                b = s - 1
                sp.wait_ge(roped, len(ROPE) * b + 1)
                alone(sp)
                need(sp, s_acc, CHUNKS * b)
                if first(b):
                    sp.wait_ge(zeroed, K_ZERO)
                alone(sp)
                for g in range(GROUPS):
                    if embed and g == 1:
                        load_x(s, 2, par)
                    for e in range(PER):
                        at = (g * PER + e) * TOK
                        sp.dma_start(k_diag[Q * e:Q * e + Q, at:at + TOK],
                                     qk[Q * g:Q * g + Q, 0:TOK]).then_inc(k_spread, 16)
            first_step()
            run_steps(sp, step, lambda: step(BATCHES, False, True))
            store(BATCHES - 1, (BATCHES - 1) % 2)
            sp.wait_ge(out_stored, 16 * NT * BATCHES)

        @block.tensor
        def _(pe):
            def x_turn(s, n):
                j, half = n // 2, n % 2
                par = (NT * parity_of[0] + j) % 2
                pe.wait_ge(x_normed, NT * s + j + 1)
                if n < 2:
                    need(pe, xT_lo_s, 6 * s)
                    need(pe, fT_lo_s, NT * (s - 1))
                else:
                    pe.wait_ge(xT_lo_s, 6 * s + n - 1)
                m = TILES[j][1]
                for k in range(HALF):
                    at = (half * HALF + k) * P
                    mm = nc.tensor.transpose(x_bank[half][:, k * P:k * P + m], x_tile[0:m, par, at:at + P], ident[0:m, 0:m])
                mm.then_inc(x_turned, 1)

            def split_product(bank, m, lhs, rhs, first, last, dep=None):
                (lh, ll), (rh, rl) = lhs, rhs
                nc.tensor.matmul(bank, lh, rh, start=first, stop=False)
                nc.tensor.matmul(bank, lh, rl, start=False, stop=False)
                return nc.tensor.matmul(bank, ll, rh, start=False, stop=last)

            def x_product(s, n):
                j, half, slot = n // 2, n % 2, n % 3
                m = TILES[j][1]
                pe.wait_ge(xT_lo_s, 6 * s + n + 1)
                if half == 0:
                    if first(s):
                        if j == 2:
                            pe.wait_ge(y_out, 1)
                    elif j == 0:
                        if first(s - 1):
                            pe.wait_ge(wf_lo_s, KH)
                        need(pe, out_ready, NT * (s - 2) + 2)
                    else:
                        pe.wait_ge(qkv_out, QKV * (s - 1) + (6 if j == 1 else 5))
                for k in range(HALF):
                    kk = half * HALF + k
                    mm = split_product(y_bank(s, j)[0:m, :], m, (act_hi[:, slot, k, 0:m], act_lo[:, slot, k, 0:m]),
                                       (w_hi[:, kk, :], w_lo[:, kk, :]), kk == 0, kk == KX - 1)
                mm.then_inc(x_used, 1)

            def h_turn(s, j):
                m = TILES[j][1]
                pe.wait_ge(h_normed, NT * s + j + 1)
                if j == 0:
                    need(pe, v_spread, CHUNK * s)
                else:
                    pe.wait_ge(hT_lo_s, NT * s + j)
                for k in range(KH):
                    mm = nc.tensor.transpose(turn_bank[:, k * P:k * P + m], norm1[0:m, k * P:(k + 1) * P], ident[0:m, 0:m])
                mm.then_inc(h_turned, 1)

            def qkv_block(b, n):
                if n == 0:
                    pe.wait_ge(hT_lo_s, NT * b + NT)
                    pe.wait_ge(y_out, NT * b + NT)
                elif n == 1:
                    pe.wait_ge(y_out, NT * b + NT - 1)
                else:
                    pe.wait_ge(qkv_out, QKV * b + n - 1)
                for k in range(KH):
                    cols = slice(n * P, (n + 1) * P)
                    mm = split_product(acc[n % 2][:, 0:TOK], P, (wqkv_hi[:, k, cols], wqkv_lo[:, k, cols]),
                                       (hT_hi[:, k, :], hT_lo[:, k, :]), k == 0, k == KH - 1)
                mm.then_inc(qkv_acc, 1)

            def v_turn(b):
                pe.wait_ge(qkv_out, QKV * b + 2)
                pe.wait_ge(hT_lo_s, NT * b + NT)
                for c in range(CHUNKS):
                    mm = nc.tensor.transpose(turn_bank[:, c * P:(c + 1) * P], 
                                             vT[:, c * CHUNK:(c + 1) * CHUNK, :].rearrange("p s q -> p (s q)"), ident[:])
                mm.then_inc(v_turned, 1)

            def scores(b, c, embed):
                if c == 0:
                    pe.wait_ge(roped, len(ROPE) * b + 2)
                    pe.wait_ge(k_spread, 16 * GROUPS * PER * (b + 1))
                if c == 0 and first(b):
                    pe.wait_ge(wf_lo_s, KH)
                    pe.wait_ge(f_bias_ready, 1)
                if c == 0 and embed:
                    pe.wait_ge(y_out, NT * (b + 1) + 1)
                if c < 2:
                    need(pe, out_ready, NT * (b - 1) + 2 + c)
                else:
                    pe.wait_ge(s_masked, CHUNKS * b + c - 1)
                for g in range(GROUPS):
                    if c == 0 and g == 2:
                        pe.wait_ge(roped, len(ROPE) * b + 3)
                    for q in range(CHUNK):
                        tok = c * CTOK + q * SEQ
                        mm = nc.tensor.matmul(s_bank[c % 2][Q * q:Q * q + Q, g * P:(g + 1) * P],
                                              qk[:, (1 + g) * TOK + tok:(1 + g) * TOK + tok + Q],
                                              wide(k_diag, g * PER * TOK + tok, TOK, PER), start=True, stop=True)
                mm.then_inc(s_acc, 1)

            def values(b, c):
                pe.wait_ge(p_turned, CHUNKS * b + c + 1)
                if c == 0:
                    pe.wait_ge(v_spread, CHUNK * (b + 1))
                need(pe, o_turned, CHUNKS * b + c)
                for g in range(GROUPS):
                    mm = nc.tensor.matmul(o_bank[:, g * P:(g + 1) * P],
                                          probT[:, c % 2, g * PER:(g + 1) * PER, :].rearrange("p a q -> p (a q)"),
                                          v_diag[:, c, g, :, :].rearrange("p a d -> p (a d)"), start=True, stop=True)
                mm.then_inc(pv_acc, 1)

            def wo_tile(b, j):
                t, m = TILES[j]
                if first(b) and j == 0:
                    pe.wait_ge(wo_lo_s, 1)
                pe.wait_ge(oT_lo_s, CHUNKS * b + -(-(t + m) // CTOK))
                if j < 2:
                    pe.wait_ge(s_masked, CHUNKS * b + 3 + j)
                else:
                    pe.wait_ge(h2_ready, NT * b + 1)
                for k in range(KH):
                    mm = split_product(s_bank[j % 2][0:m, :], m, (oT_hi[:, k, t:t + m], oT_lo[:, k, t:t + m]),
                                       (wo_hi[:, k, :], wo_lo[:, k, :]), k == 0, k == KH - 1)
                mm.then_inc(wo_acc, 1)

            def f_turn(s, b, j, embed):
                m = TILES[j][1]
                pe.wait_ge(h2_normed, NT * b + j + 1)
                if j == 2:
                    pe.wait_ge(fT_lo_s, NT * b + 1)
                elif embed:
                    pe.wait_ge(xT_lo_s, 6 * s + 6)
                else:
                    pe.wait_ge(fT_lo_s, NT * b)
                for k in range(KH):
                    mm = nc.tensor.transpose(x_bank[j % 2][:, k * P:k * P + m], norm2[0:m, k * P:(k + 1) * P], ident[0:m, 0:m])
                mm.then_inc(f_turned, 1)

            def f_tile(b, j):
                m = TILES[j][1]
                pe.wait_ge(fT_lo_s, NT * b + j + 1)
                pe.wait_ge(*((h2_ready, NT * b + 2 + j) if j < 2 else (out_ready, NT * b + 1)))
                for k in range(KH):
                    mm = split_product(s_bank[1 - j % 2][0:m, :], m, (act_hi[:, j, k, 0:m], act_lo[:, j, k, 0:m]),
                                       (wf_hi[:, k, :], wf_lo[:, k, :]), k == 0, k == KH - 1)
                mm.then_inc(f_acc, 1)

            def ffn_weights(u):
                o, half = u // 2, u % 2
                pe.wait_ge(*{5: (unit_diff_dve, 1), 6: (unit_diff, 6), 7: (unit_diff_dve, 2)}.get(u, (unit_diff, u + 1)))
                if u == 0:
                    pe.wait_ge(gate_ready, 1)
                if half == 0 and o >= 2:
                    pe.wait_ge(wf_lo_s, o - 1)
                diff = unit_p[u % 4].rearrange("p (i n) -> p i n", n=BITS)
                for kk in range(2):
                    k = 2 * half + kk
                    for n in range(BITS):
                        mm = nc.tensor.matmul(s_bank[o % 2][:, k * P:(k + 1) * P], diff[:, kk * P:(kk + 1) * P, n],
                                              gate_diag[:, n, :], start=(n == 0), stop=(n == BITS - 1))
                mm.then_inc(unit_used, 1)

            def beta_product(half):
                if half == 0:
                    pe.wait_ge(b1_wide_ready, 1)
                for k in range(half * KX // 2, (half + 1) * KX // 2):
                    if k % 2 == 0:
                        pe.wait_ge(w_here[k // 2], 16)
                    mm = nc.tensor.matmul(o_bank[:], b1_wide[:, k, :], w_raw[:, k, :], start=(k == 0), stop=(k == KX - 1))
                return mm

            def first_step():
                pe.wait_ge(const_step, CONSTS)
                x_turn(0, 0)
                x_turn(0, 1)
                beta_product(0)
                pe.wait_ge(w_lo_s, KX // 2)
                x_product(0, 0)
                x_turn(0, 2)
                beta_product(1).then_inc(y_const, 1)
                pe.wait_ge(w_lo_s, KX)
                x_product(0, 1)
                x_turn(0, 3)
                x_product(0, 2)
                ffn_weights(0)
                x_product(0, 3)
                x_turn(0, 4)
                x_turn(0, 5)
                x_product(0, 4)
                ffn_weights(1)
                x_product(0, 5)
                h_turn(0, 0)
                ffn_weights(2)
                pe.wait_ge(f_diag_ready, 1)
                pe.wait_ge(y_bias_ready, 1)
                nc.tensor.matmul(o_bank[:], ones, f_diag.rearrange("p k q -> p (k q)"), start=True, stop=True).then_inc(f_bias_acc, 1)
                h_turn(0, 1)
                ffn_weights(3)
                ffn_weights(4)
                h_turn(0, 2)
                for u in range(5, UNITS):
                    ffn_weights(u)
                pe.wait_ge(wqkv_lo_s, 2)

            parity_of = [0]

            def step(s, embed, attend, parity=None):
                parity_of[0] = s % 2 if parity is None else parity
                b = s - 1
                if attend:
                    qkv_block(b, 0)
                    qkv_block(b, 1)
                    qkv_block(b, 2)
                    qkv_block(b, 3)
                if embed:
                    x_turn(s, 0)
                    x_turn(s, 1)
                if attend:
                    qkv_block(b, 4)
                    qkv_block(b, 5)
                if embed:
                    x_product(s, 0)
                    x_product(s, 1)
                    x_turn(s, 2)
                if attend:
                    v_turn(b)
                if embed:
                    x_turn(s, 3)
                if attend:
                    scores(b, 0, embed)
                    scores(b, 1, embed)
                    scores(b, 2, embed)
                if embed:
                    x_turn(s, 4)
                    x_product(s, 2)
                if attend:
                    scores(b, 3, embed)
                if embed:
                    x_turn(s, 5)
                if attend:
                    values(b, 0)
                if embed:
                    x_product(s, 3)
                if attend:
                    values(b, 1)
                if embed:
                    x_product(s, 4)
                if attend:
                    values(b, 2)
                    wo_tile(b, 0)
                if embed:
                    h_turn(s, 0)
                if attend:
                    wo_tile(b, 1)
                    values(b, 3)
                if embed:
                    x_product(s, 5)
                if attend:
                    f_turn(s, b, 0, embed)
                    wo_tile(b, 2)
                if embed:
                    h_turn(s, 1)
                if attend:
                    f_turn(s, b, 1, embed)
                    f_tile(b, 0)
                    f_turn(s, b, 2, embed)
                    f_tile(b, 1)
                if embed:
                    h_turn(s, 2)
                if attend:
                    f_tile(b, 2)

            def last_step():
                s, b, embed = BATCHES, BATCHES - 1, False
                parity_of[0] = s % 2
                qkv_block(b, 0)
                qkv_block(b, 1)
                qkv_block(b, 2)
                qkv_block(b, 3)
                v_turn(b)
                qkv_block(b, 4)
                qkv_block(b, 5)
                scores(b, 0, embed)
                scores(b, 1, embed)
                scores(b, 2, embed)
                values(b, 0)
                scores(b, 3, embed)
                values(b, 1)
                values(b, 2)
                wo_tile(b, 0)
                values(b, 3)
                wo_tile(b, 1)
                f_turn(s, b, 0, embed)
                wo_tile(b, 2)
                f_turn(s, b, 1, embed)
                f_tile(b, 0)
                f_turn(s, b, 2, embed)
                f_tile(b, 1)
                f_tile(b, 2)

            first_step()
            run_steps(pe, step, last_step)

        @block.scalar
        def _(act):
            def split_hi(dst, bank, m):
                return nc.scalar.activation(dst[:, :, 0:m], bank[:].rearrange("p (k t) -> p k t", k=HALF)[:, :, 0:m], ACT.Copy)

            def normalise(dst, src, m, key, ready, count, done):
                act.wait_ge(ready, count)
                nc.scalar.activation(dst, src, ACT.Identity, scale=mo[key][0:m, 3:4], bias=mo[key][0:m, 4:5]).then_inc(done, 1)

            def x_normalise(s, j, par):
                m = TILES[j][1]
                t = x_tile[0:m, (NT * par + j) % 2, :]
                normalise(t, t, m, "x", x_rstd, NT * s + j + 1, x_normed)

            def x_high(s, n):
                act.wait_ge(x_turned, 6 * s + n + 1)
                if n < 3:
                    need(act, f_acc, NT * (s - 2) + NT + n - 2)
                    need(act, x_used, 6 * s - 3 + n)
                else:
                    act.wait_ge(x_used, 6 * s + n - 2)
                split_hi(act_hi[:, n % 3], x_bank[n % 2], TILES[n // 2][1]).then_inc(xT_hi_s, 1)

            def qkv_evacuate(b, n):
                act.wait_ge(qkv_acc, QKV * b + n + 1)
                need(act, s_acc, CHUNKS * b)
                if n == 1:
                    dst = vT[:, :, 0:SEQ]
                    need(act, f_turned, NT * b)
                    need(act, v_turned, b)
                else:
                    at = max(n - 1, 0) * TOK
                    dst = qk[:, at:at + TOK]
                src = acc[n % 2][:, 0:TOK]
                if n == 1:
                    src = src.rearrange("p (s q) -> p s q", q=SEQ)
                nc.scalar.activation(dst, src, ACT.Identity, bias=qkv_bias[:, n:n + 1]).then_inc(qkv_out, 1)

            def spread_values(b):
                act.wait_ge(v_turned, b + 1)
                need(act, pv_acc, CHUNKS * b)
                if first(b):
                    act.wait_ge(zeroed, V_ZERO)
                for q in range(CHUNK):
                    rows = slice(Q * q, Q * q + Q)
                    nc.scalar.activation(v_diag[rows, :, :, q, :].rearrange("p c g d -> p (c g) d"),
                                         turn_bank[rows, :].rearrange("p (c d) -> p c d", d=Q), ACT.Copy).then_inc(v_spread, 1)

            def exponentials(b, c):
                act.wait_ge(s_shifted, CHUNKS * b + c + 1)
                nc.scalar.activation(prob[:, c % 2, :, 0:SEQ], prob[:, c % 2, :, 0:SEQ], ACT.Exp, scale=SCALE).then_inc(p_exp, 1)

            def h_normalise(s, j):
                m = TILES[j][1]
                need(act, h_turned, NT * s + j)
                normalise(norm1[0:m, :], h[0:m, par_now[0], j, :], m, "h", h_rstd, NT * s + j + 1, h_normed)

            def h_high(s, j):
                t, m = TILES[j]
                act.wait_ge(h_turned, NT * s + j + 1)
                need(act, qkv_acc, QKV * s)
                split_hi(hT_hi[:, :, t:t + m], turn_bank, m).then_inc(hT_hi_s, 1)

            def o_high(b, c):
                act.wait_ge(o_turned, CHUNKS * b + c + 1)
                need(act, wo_acc, NT * b)
                nc.scalar.activation(heads_of(oT_hi, c), oT[:, :, :, 0:SEQ], ACT.Copy).then_inc(oT_hi_s, 1)

            def f_normalise(b, j):
                m = TILES[j][1]
                need(act, f_turned, NT * b + j)
                act.wait_ge(v_turned, b + 1)
                normalise(norm2[0:m, :], h[0:m, 1 - par_now[0], j, :], m, "f", h2_rstd, NT * b + j + 1, h2_normed)

            def f_high(s, b, j, embed):
                act.wait_ge(f_turned, NT * b + j + 1)
                if embed:
                    act.wait_ge(x_used, 6 * s + 4 + j)
                else:
                    act.wait_ge(f_acc, NT * (b - 1) + j + 1)
                split_hi(act_hi[:, j], x_bank[j % 2], TILES[j][1]).then_inc(fT_hi_s, 1)

            def w_high(k):
                if k % 2 == 0:
                    act.wait_ge(w_here[k // 2], 16)
                nc.scalar.activation(w_hi[:, k, :], w_raw[:, k, :], ACT.Copy, scale=g1_col[:, k:k + 1]).then_inc(w_hi_s, 1)

            def wqkv_high(i):
                act.wait_ge(wqkv_here[i], 16)
                nc.scalar.activation(wqkv_hi[:, 2 * i:2 * i + 2, :], wqkv_raw[i], ACT.Copy).then_inc(wqkv_hi_s, 1)

            def gate_unit(u):
                act.wait_ge(unit_here[u % 4], 32 * (u // 4 + 1))
                nc.scalar.activation(unit_p[u % 4], unit_p[u % 4], ACT.Sigmoid).then_inc(unit_gated, 1)
                nc.scalar.activation(unit_n[u % 4], unit_n[u % 4], ACT.Sigmoid).then_inc(unit_gated, 1)

            def wf_high(o):
                act.wait_ge(unit_used, 2 * o + 2)
                nc.scalar.activation(wf_hi[:, :, o * P:(o + 1) * P], s_bank[o % 2][:].rearrange("p (k t) -> p k t", t=P),
                                     ACT.Copy).then_inc(wf_hi_s, 1)

            def first_step():
                act.dma_start(columns, columns_in).then_inc(columns_here, 16)
                act.dma_start(gates, gates_in.partition_broadcast(P)).then_inc(gates_here, 16)
                act.dma_start(rows_all[:].rearrange("p a n -> p (a n)"), rows_in.partition_broadcast(P)).then_inc(rows_here, 16)
                act.dma_start(qkv_bias[:], qkv_bias_in).then_inc(qkv_bias_here, 16)
                act.dma_start(tables[:].rearrange("p a n -> p (a n)"), tables_in).then_inc(tables_here, 16)
                x_normalise(0, 0, 0)
                act.wait_ge(columns_here, 16)
                w_high(0)
                w_high(1)
                x_high(0, 0)
                x_high(0, 1)
                for k in range(2, KX):
                    w_high(k)
                x_normalise(0, 1, 0)
                x_high(0, 2)
                act.wait_ge(gates_here, 16)
                nc.scalar.activation(gate, gate, ACT.Sigmoid).then_inc(gate_sig, 1)
                gate_unit(0)
                wqkv_high(0)
                x_high(0, 3)
                x_normalise(0, 2, 0)
                wqkv_high(1)
                gate_unit(1)
                x_high(0, 4)
                x_high(0, 5)
                gate_unit(2)
                h_normalise(0, 0)
                act.wait_ge(wo_here, 16)
                nc.scalar.activation(wo_hi[:], wo_raw, ACT.Copy).then_inc(wo_hi_s, 1)
                gate_unit(3)
                h_high(0, 0)
                gate_unit(4)
                h_normalise(0, 1)
                wf_high(0)
                gate_unit(5)
                h_high(0, 1)
                gate_unit(6)
                wf_high(1)
                h_normalise(0, 2)
                h_high(0, 2)
                gate_unit(7)
                wf_high(2)
                wf_high(3)
                act.wait_ge(qkv_bias_here, 16)

            par_now = [0]

            def step(s, embed, attend, parity=None):
                par = par_now[0] = s % 2 if parity is None else parity
                b = s - 1
                if attend:
                    qkv_evacuate(b, 0)
                    qkv_evacuate(b, 1)
                if embed:
                    x_normalise(s, 0, par)
                if attend:
                    qkv_evacuate(b, 2)
                    qkv_evacuate(b, 3)
                if embed:
                    x_high(s, 0)
                    x_normalise(s, 1, par)
                if attend:
                    qkv_evacuate(b, 4)
                if embed:
                    x_high(s, 1)
                if attend:
                    qkv_evacuate(b, 5)
                if embed:
                    x_high(s, 2)
                if attend:
                    spread_values(b)
                if embed:
                    x_normalise(s, 2, par)
                if attend:
                    exponentials(b, 0)
                if embed:
                    x_high(s, 3)
                    x_high(s, 4)
                if attend:
                    exponentials(b, 1)
                if embed:
                    x_high(s, 5)
                if attend:
                    o_high(b, 0)
                    exponentials(b, 2)
                if embed:
                    h_normalise(s, 0)
                if attend:
                    o_high(b, 1)
                    exponentials(b, 3)
                    o_high(b, 2)
                    f_normalise(b, 0)
                if embed:
                    h_high(s, 0)
                if attend:
                    o_high(b, 3)
                    f_high(s, b, 0, embed)
                if embed:
                    h_normalise(s, 1)
                if attend:
                    f_normalise(b, 1)
                    f_high(s, b, 1, embed)
                    f_normalise(b, 2)
                    f_high(s, b, 2, embed)
                if embed:
                    h_high(s, 1)
                    h_normalise(s, 2)
                    h_high(s, 2)

            def last_step():
                s, b, embed = BATCHES, BATCHES - 1, False
                par_now[0] = s % 2
                qkv_evacuate(b, 0)
                qkv_evacuate(b, 1)
                qkv_evacuate(b, 2)
                qkv_evacuate(b, 3)
                qkv_evacuate(b, 4)
                qkv_evacuate(b, 5)
                spread_values(b)
                exponentials(b, 0)
                exponentials(b, 1)
                exponentials(b, 2)
                o_high(b, 0)
                o_high(b, 1)
                exponentials(b, 3)
                o_high(b, 2)
                o_high(b, 3)
                f_normalise(b, 0)
                f_high(s, b, 0, embed)
                f_normalise(b, 1)
                f_high(s, b, 1, embed)
                f_normalise(b, 2)
                f_high(s, b, 2, embed)

            first_step()
            run_steps(act, step, last_step)

        @block.gpsimd
        def _(pool):
            def deviation(key, m, eps, moments, rstd, count):
                v = mo[key]
                pool.wait_ge(moments, count)
                alone(pool)
                nc.gpsimd.tensor_scalar(v[0:m, 2:3], v[0:m, 1:2], eps, None, ALU.add).then_inc(chain, 1)
                tick(1)
                last = key == "y"
                nc.gpsimd.tensor_tensor(v[0:m, 3:4], v[0:m, 2:3], minus_half[0:m, :], ALU.pow)\
                    .then_inc(rstd if last else chain, 1)
                if not last:
                    tick(1)
                    alone(pool)
                    nc.gpsimd.tensor_scalar(v[0:m, 4:5], v[0:m, 0:1], v[0:m, 3:4], -1.0, ALU.mult, ALU.mult).then_inc(rstd, 1)

            def tick(n):
                done[0] += n
                pool.wait_ge(chain, base[0] + done[0])

            def rope_cosine(b, n):
                first, blocks = ROPE[n]
                v = qk[:, first * TOK:(first + blocks) * TOK].rearrange("p (a t) -> p a t", t=SEQ)
                pool.wait_ge(rope_swapped, len(ROPE) * b + n + 1)
                nc.gpsimd.tensor_tensor(v, v, table(cos, blocks * BATCH), ALU.mult).then_inc(rope_cos, 1)

            def shift(b, c):
                v = prob[:, c % 2, :, 0:SEQ]
                pool.wait_ge(s_max, CHUNKS * b + c + 1)
                nc.gpsimd.tensor_tensor(v, v, row_max[:, c % 2, :].unsqueeze(2).broadcast_to([P, HEADS, SEQ]),
                                        ALU.subtract).then_inc(s_shifted, 1)

            def divide(b, c):
                v = prob[:, c % 2, :, 0:SEQ]
                pool.wait_ge(p_inv, CHUNKS * b + c + 1)
                nc.gpsimd.tensor_tensor(v, v, row_inv[:, c % 2, :].unsqueeze(2).broadcast_to([P, HEADS, SEQ]),
                                        ALU.mult).then_inc(p_scaled, 1)

            def o_low(b, c):
                pool.wait_ge(oT_hi_s, CHUNKS * b + c + 1)
                nc.gpsimd.tensor_tensor(heads_of(oT_lo, c), oT[:, :, :, 0:SEQ],
                                        heads_of(oT_hi, c).bitcast(F32), ALU.subtract).then_inc(oT_lo_s, 1)

            def add_output_bias(b, j):
                m = TILES[j][1]
                t = h[0:m, 1 - par_now[0], j, :]
                pool.wait_ge(h_normed, NT * b + j + 1)
                nc.gpsimd.tensor_tensor(t, t, bo_all[0:m, :], ALU.add).then_inc(h_biased, 1)

            def add_ffn_bias(b, j):
                m = TILES[j][1]
                t = h[0:m, 1 - par_now[0], j, :]
                pool.wait_ge(h2_normed, NT * b + j + 1)
                nc.gpsimd.tensor_tensor(t, t, f_bias[0:m, :], ALU.add).then_inc(out_biased, 1)

            def x_dev(s, j):
                deviation("x", TILES[j][1], EPS_TOK, x_moments, x_rstd, NT * s + j + 1)

            def y_dev(s, j):
                deviation("y", TILES[j][1], EPS_TOK, y_moments, y_rstd, NT * s + j + 1)

            def h_dev(s, j):
                deviation("h", TILES[j][1], EPS_LN, h_moments, h_rstd, NT * s + j + 1)

            def f_dev(b, j):
                deviation("f", TILES[j][1], EPS_LN, h2_moments, h2_rstd, NT * b + j + 1)

            par_now, done, base = [0], [0], [0]
            EMBED_STEPS, ATTEND_STEPS = NT * (2 + 1 + 2), NT * 2

            def step(s, embed, attend, parity=None):
                par_now[0] = s % 2 if parity is None else parity
                b = s - 1
                done[0] = 0
                base[0] = EMBED_STEPS * s + (ATTEND_STEPS * b if attend else 0)

                if embed:
                    x_dev(s, 0)
                if attend:
                    rope_cosine(b, 0)
                    add_output_bias(b, 0)
                if embed:
                    x_dev(s, 1)
                if attend:
                    rope_cosine(b, 1)
                    rope_cosine(b, 2)
                    add_output_bias(b, 1)
                if embed:
                    x_dev(s, 2)
                    y_dev(s, 0)
                if attend:
                    shift(b, 0)
                    shift(b, 1)
                    divide(b, 0)
                if embed:
                    h_dev(s, 0)
                if attend:
                    divide(b, 1)
                    shift(b, 2)
                    o_low(b, 0)
                    divide(b, 2)
                    o_low(b, 1)
                    shift(b, 3)
                if embed:
                    y_dev(s, 1)
                if attend:
                    o_low(b, 2)
                    divide(b, 3)
                    f_dev(b, 0)
                if embed:
                    h_dev(s, 1)
                if attend:
                    o_low(b, 3)
                    f_dev(b, 1)
                    add_output_bias(b, 2)
                if embed:
                    y_dev(s, 2)
                if attend:
                    f_dev(b, 2)
                    add_ffn_bias(b, 0)
                if embed:
                    h_dev(s, 2)
                if attend:
                    add_ffn_bias(b, 1)
                    add_ffn_bias(b, 2)

            def last_step():
                s, b = BATCHES, BATCHES - 1
                par_now[0], done[0] = s % 2, 0
                base[0] = EMBED_STEPS * s + ATTEND_STEPS * b
                rope_cosine(b, 0)
                add_output_bias(b, 0)
                rope_cosine(b, 1)
                rope_cosine(b, 2)
                shift(b, 0)
                shift(b, 1)
                divide(b, 0)
                divide(b, 1)
                shift(b, 2)
                add_output_bias(b, 1)
                o_low(b, 0)
                divide(b, 2)
                shift(b, 3)
                o_low(b, 1)
                divide(b, 3)
                o_low(b, 2)
                f_dev(b, 0)
                o_low(b, 3)
                add_output_bias(b, 2)
                f_dev(b, 1)
                add_ffn_bias(b, 0)
                f_dev(b, 2)
                add_ffn_bias(b, 1)
                add_ffn_bias(b, 2)

            def unit_difference(u):
                pool.wait_ge(unit_gated, 2 * u + 2)
                nc.gpsimd.tensor_tensor(unit_p[u % 4], unit_p[u % 4], unit_n[u % 4], ALU.subtract).then_inc(unit_diff, 1)

            def first_step():
                nc.gpsimd.memset(ident[:], 0.0).then_inc(const_step, 1)
                nc.gpsimd.memset(minus_half[:], -0.5).then_inc(const_step, 1)
                nc.gpsimd.memset(ones, 1.0).then_inc(const_step, 1)
                pool.wait_ge(const_step, CONSTS - 1)
                nc.gpsimd.affine_select(out=ident[:], in_=ident[:], compare_op=ALU.not_equal, fill=1.0, base=0,
                                        pattern=[[-1, P]], channel_multiplier=1).then_inc(const_step, 1)
                pool.wait_ge(const_step, CONSTS)
                nc.gpsimd.memset(qk[:, (1 + KH) * TOK:], 0.0).then_inc(zeroed, 1)
                x_dev(0, 0)
                x_dev(0, 1)
                pool.wait_ge(gate_sig, 1)
                nc.gpsimd.tensor_tensor(gate, gate, exps, ALU.mult).then_inc(gate_step, 1)
                pool.wait_ge(gate_step, 1)
                nc.gpsimd.tensor_tensor(gate, gate, scale.broadcast_to([P, BITS]), ALU.mult).then_inc(gate_step, 1)
                pool.wait_ge(gate_step, 2)
                nc.gpsimd.tensor_tensor(gate_diag, ident[:].unsqueeze(1).broadcast_to([P, BITS, P]),
                                        gate.unsqueeze(2).broadcast_to([P, BITS, P]), ALU.mult).then_inc(gate_ready, 1)
                x_dev(0, 2)
                unit_difference(0)
                y_dev(0, 0)
                unit_difference(1)
                h_dev(0, 0)
                y_dev(0, 1)
                unit_difference(2)
                h_dev(0, 1)
                unit_difference(3)
                y_dev(0, 2)
                unit_difference(4)
                h_dev(0, 2)
                unit_difference(6)
                pool.wait_ge(wo_lo_s, 1)
                nc.gpsimd.memset(v_diag[:], 0.0).then_inc(zeroed, 1)
                pool.wait_ge(unit_diff, 5)
                nc.gpsimd.memset(prob[:, :, :, SEQ:], 0.0).then_inc(zeroed, 1)
                pool.wait_ge(unit_used, UNITS - 1)
                nc.gpsimd.memset(k_diag[:, 0:W_LEN], 0.0).then_inc(zeroed, 1)
                pool.wait_ge(unit_used, UNITS)
                pool.wait_ge(f_bias_acc, 1)
                nc.gpsimd.memset(k_diag[:, W_LEN:], 0.0).then_inc(zeroed, 1)

            first_step()
            run_steps(pool, step, last_step)

        @block.vector
        def _(dve):
            def moments(key, src, m, done, count):
                n = src.shape[-1] // 512
                for i in range(n):
                    ins = nc.vector.bn_stats(stats[0:m, 0 if key != "x" else i, :] if key == "x" else stats_of[key][0:m, :],
                                             src[:, i * 512:(i + 1) * 512]).then_inc(st[key], 1)
                dve.wait_ge(st[key], count * n)
                src6 = stats[0:m, 0:2, :].rearrange("p a b -> p (a b)") if key == "x" else stats_of[key][0:m, :]
                alone(dve)
                nc.vector.bn_aggr(mo[key][0:m, 0:2], src6).then_inc(done, 1)

            def x_stats(s, j, par):
                m = TILES[j][1]
                dve.wait_ge(x_loaded[j], 16 * len(pieces(j)) * (s + 1))
                need(dve, x_normed, NT * s + j)
                moments("x", x_tile[0:m, (NT * par + j) % 2, :], m, x_moments, NT * s + j + 1)

            def split_lo(dst, bank, hi, m):
                return nc.vector.tensor_tensor(dst[:, :, 0:m], bank[:].rearrange("p (k t) -> p k t", k=HALF)[:, :, 0:m],
                                               hi[:, :, 0:m].bitcast(F32), ALU.subtract)

            def x_low(s, n):
                dve.wait_ge(xT_hi_s, 6 * s + n + 1)
                split_lo(act_lo[:, n % 3], x_bank[n % 2], act_hi[:, n % 3], TILES[n // 2][1]).then_inc(xT_lo_s, 1)

            def rope_part(b, n):
                first, blocks = ROPE[n]
                at = max(first - 1, 0) * TOK
                return qk[:, first * TOK:(first + blocks) * TOK], swapped[:, at:at + blocks * TOK], blocks

            def rope_sine(b, n):
                v, w, blocks = rope_part(b, n)
                dve.wait_ge(qkv_out, QKV * b + (1 if n == 0 else 2 * n + 2))
                if n == 0:
                    need(dve, pv_acc, CHUNKS * b)
                    need(dve, oT_lo_s, CHUNKS * b)
                if n == 1:
                    dve.wait_ge(roped, len(ROPE) * b + 1)
                alone(dve)
                nc.vector.stream_shuffle(w, v, [(i + HEAD // 2) % Q for i in range(Q)]).then_inc(rope_swapped, 1)
                dve.wait_ge(rope_swapped, len(ROPE) * b + n + 1)
                w3 = w.rearrange("p (a t) -> p a t", t=SEQ)
                nc.vector.tensor_tensor(w3, w3, table(sin, blocks * BATCH), ALU.mult).then_inc(rope_sin, 1)

            def rope_sum(b, n):
                v, w, blocks = rope_part(b, n)
                dve.wait_ge(rope_sin, len(ROPE) * b + n + 1)
                dve.wait_ge(rope_cos, len(ROPE) * b + n + 1)
                nc.vector.tensor_tensor(v, v, w, ALU.add).then_inc(roped, 1)

            def y_evacuate(s, j):
                m = TILES[j][1]
                t = h[0:m, par_now[0], j, :]
                dve.wait_ge(x_used, 6 * s + 2 * j + 2)
                need(dve, out_stored, 16 * (NT * (s - 2) + NT))
                nc.vector.tensor_tensor(t, y_bank(s, j)[0:m, :], y_bias[0:m, :], ALU.add).then_inc(y_out, 1)
                dve.wait_ge(y_out, NT * s + j + 1)
                need(dve, h_ready, NT * s + j)
                moments("y", t, m, y_moments, NT * s + j + 1)

            def y_centre(s, j):
                m = TILES[j][1]
                t = h[0:m, par_now[0], j, :]
                dve.wait_ge(y_moments, NT * s + j + 1)
                nc.vector.scalar_tensor_tensor(out=t, in0=t, scalar=mo["y"][0:m, 0:1], in1=g2_all[0:m, :],
                                               op0=ALU.subtract, op1=ALU.mult).then_inc(h_gained, 1)

            def y_scale(s, j):
                m = TILES[j][1]
                t = h[0:m, par_now[0], j, :]
                dve.wait_ge(y_rstd, NT * s + j + 1)
                dve.wait_ge(h_gained, NT * s + j + 1)
                nc.vector.scalar_tensor_tensor(out=t, in0=t, scalar=mo["y"][0:m, 3:4], in1=b2_all[0:m, :],
                                               op0=ALU.mult, op1=ALU.add).then_inc(h_ready, 1)

            def mask_scores(b, c):
                v = prob[:, c % 2, :, 0:SEQ]
                dve.wait_ge(s_acc, CHUNKS * b + c + 1)
                need(dve, p_turned, CHUNKS * b + c - 1)
                if first(b) and c == 0:
                    dve.wait_ge(zeroed, PROB_ZERO)
                nc.vector.tensor_tensor(v, s_bank[c % 2][:].rearrange("p (a k) -> p a k", k=Q)[:, :, 0:SEQ],
                                        mask.unsqueeze(1).broadcast_to([P, HEADS, SEQ]), ALU.add).then_inc(s_masked, 1)
                dve.wait_ge(s_masked, CHUNKS * b + c + 1)
                nc.vector.tensor_reduce(row_max[:, c % 2, :], v, AX_X, ALU.max).then_inc(s_max, 1)

            def sum_up(b, c):
                dve.wait_ge(p_exp, CHUNKS * b + c + 1)
                need(dve, p_scaled, CHUNKS * b + c - 1)
                nc.vector.tensor_reduce(row_sum[:, c % 2, :], prob[:, c % 2, :, 0:SEQ], AX_X, ALU.add).then_inc(p_sum, 1)
                dve.wait_ge(p_sum, CHUNKS * b + c + 1)
                nc.vector.reciprocal(row_inv[:, c % 2, :], row_sum[:, c % 2, :]).then_inc(p_inv, 1)

            def turn_probs(b, c):
                dve.wait_ge(p_scaled, CHUNKS * b + c + 1)
                need(dve, pv_acc, CHUNKS * b + c - 1)
                if c == 0:
                    dve.wait_ge(roped, len(ROPE) * (b + 1))
                nc.vector.transpose(probT[:, c % 2].rearrange("p a q -> p (a q)"),
                                    prob[:, c % 2].rearrange("p a q -> p (a q)")).then_inc(p_turned, 1)

            def turn_heads(b, c):
                dve.wait_ge(pv_acc, CHUNKS * b + c + 1)
                need(dve, oT_hi_s, CHUNKS * b + c)
                need(dve, oT_lo_s, CHUNKS * b + c)
                nc.vector.transpose(oT.rearrange("p g s q -> p (g s q)"), o_bank[:]).then_inc(o_turned, 1)

            def h_stats(s, j):
                m = TILES[j][1]
                dve.wait_ge(h_ready, NT * s + j + 1)
                need(dve, h_normed, NT * s + j)
                moments("h", h[0:m, par_now[0], j, :], m, h_moments, NT * s + j + 1)

            def h_low(s, j):
                t, m = TILES[j]
                dve.wait_ge(hT_hi_s, NT * s + j + 1)
                split_lo(hT_lo[:, :, t:t + m], turn_bank, hT_hi[:, :, t:t + m], m).then_inc(hT_lo_s, 1)

            def add_attention(b, j):
                m = TILES[j][1]
                t = h[0:m, 1 - par_now[0], j, :]
                dve.wait_ge(wo_acc, NT * b + j + 1)
                dve.wait_ge(h_biased, NT * b + j + 1)
                nc.vector.tensor_tensor(t, s_bank[j % 2][0:m, :], t, ALU.add).then_inc(h2_ready, 1)
                dve.wait_ge(h2_ready, NT * b + j + 1)
                need(dve, h2_normed, NT * b + j)
                moments("f", t, m, h2_moments, NT * b + j + 1)

            def f_low(b, j):
                dve.wait_ge(fT_hi_s, NT * b + j + 1)
                split_lo(act_lo[:, j], x_bank[j % 2], act_hi[:, j], TILES[j][1]).then_inc(fT_lo_s, 1)

            def add_ffn(b, j):
                m = TILES[j][1]
                t = h[0:m, 1 - par_now[0], j, :]
                dve.wait_ge(f_acc, NT * b + j + 1)
                dve.wait_ge(out_biased, NT * b + j + 1)
                nc.vector.tensor_tensor(t, s_bank[1 - j % 2][0:m, :], t, ALU.add).then_inc(out_ready, 1)

            def w_low(k):
                dve.wait_ge(w_hi_s, k + 1)
                nc.vector.scalar_tensor_tensor(out=w_lo[:, k, :], in0=w_raw[:, k, :], scalar=g1_col[:, k:k + 1],
                                               in1=w_hi[:, k, :].bitcast(F32), op0=ALU.mult, op1=ALU.subtract).then_inc(w_lo_s, 1)

            def wqkv_low(i):
                dve.wait_ge(wqkv_hi_s, i + 1)
                nc.vector.tensor_tensor(wqkv_lo[:, 2 * i:2 * i + 2, :], wqkv_raw[i],
                                        wqkv_hi[:, 2 * i:2 * i + 2, :].bitcast(F32), ALU.subtract).then_inc(wqkv_lo_s, 1)

            def wf_low(o):
                dve.wait_ge(wf_hi_s, o + 1)
                cols = slice(o * P, (o + 1) * P)
                nc.vector.tensor_tensor(wf_lo[:, :, cols], s_bank[o % 2][:].rearrange("p (k t) -> p k t", t=P),
                                        wf_hi[:, :, cols].bitcast(F32), ALU.subtract).then_inc(wf_lo_s, 1)

            def unit_difference(u):
                dve.wait_ge(unit_gated, 2 * u + 2)
                nc.vector.tensor_tensor(unit_p[u % 4], unit_p[u % 4], unit_n[u % 4], ALU.subtract).then_inc(unit_diff_dve, 1)

            def ffn_bias_columns():
                steps = [0]

                def after(ins):
                    steps[0] += 1
                    ins.then_inc(f_step, 1)
                    dve.wait_ge(f_step, steps[0])

                dve.wait_ge(gates_here, 16)
                after(nc.vector.tensor_tensor(pbias, pbias, nbias, ALU.subtract))
                d3 = pbias.rearrange("p (k n) -> p k n", n=BITS)
                after(nc.vector.tensor_tensor(d3, d3, bexps.unsqueeze(1).broadcast_to([P, KH, BITS]), ALU.mult))
                after(nc.vector.tensor_reduce(f_col, d3, AX_X, ALU.add))
                after(nc.vector.tensor_scalar(f_col, f_col, 1.0, -1.0, ALU.min, ALU.max))
                after(nc.vector.tensor_scalar(f_col, f_col, STEP, ROUND, ALU.mult, ALU.add))
                after(nc.vector.tensor_scalar(f_col, f_col, ROUND, 1.0 / STEP, ALU.subtract, ALU.mult))
                after(nc.vector.tensor_scalar(f_col, f_col, biasscale, None, ALU.mult))
                nc.vector.tensor_tensor(f_diag, ident[:].unsqueeze(1).broadcast_to([P, KH, P]),
                                        f_col.unsqueeze(2).broadcast_to([P, KH, P]), ALU.mult).then_inc(f_diag_ready, 1)

            def first_step():
                dve.wait_ge(columns_here, 16)
                nc.vector.tensor_copy(b1_wide, b1_col.unsqueeze(2).broadcast_to([P, KX, P])).then_inc(b1_wide_ready, 1)
                x_stats(0, 0, 0)
                w_low(0)
                w_low(1)
                x_low(0, 0)
                x_low(0, 1)
                w_low(2)
                w_low(3)
                x_stats(0, 1, 0)
                for k in range(KX // 2, KX):
                    w_low(k)
                x_low(0, 2)
                x_stats(0, 2, 0)
                x_low(0, 3)
                dve.wait_ge(y_const, 1)
                dve.wait_ge(rows_here, 16)
                nc.vector.tensor_tensor(y_bias, o_bank[:], y_bias, ALU.add).then_inc(y_bias_ready, 1)
                dve.wait_ge(y_bias_ready, 1)
                y_evacuate(0, 0)
                wqkv_low(0)
                y_centre(0, 0)
                wqkv_low(1)
                x_low(0, 4)
                x_low(0, 5)
                y_scale(0, 0)
                h_stats(0, 0)
                y_evacuate(0, 1)
                y_centre(0, 1)
                dve.wait_ge(const_step, CONSTS)
                ffn_bias_columns()
                y_scale(0, 1)
                h_stats(0, 1)
                h_low(0, 0)
                y_evacuate(0, 2)
                y_centre(0, 2)
                wf_low(0)
                y_scale(0, 2)
                h_stats(0, 2)
                dve.wait_ge(f_bias_acc, 1)
                nc.vector.tensor_copy(f_bias[:], o_bank[:]).then_inc(f_bias_ready, 1)
                h_low(0, 1)
                unit_difference(5)
                wf_low(1)
                dve.wait_ge(wo_hi_s, 1)
                nc.vector.tensor_tensor(wo_lo[:], wo_raw, wo_hi[:].bitcast(F32), ALU.subtract).then_inc(wo_lo_s, 1)
                h_low(0, 2)
                unit_difference(7)
                for o in range(2, KH):
                    wf_low(o)
                dve.wait_ge(tables_here, 16)

            par_now = [0]

            def step(s, embed, attend, parity=None):
                par = par_now[0] = s % 2 if parity is None else parity
                b = s - 1
                if embed:
                    x_stats(s, 0, par)
                if attend:
                    rope_sine(b, 0)
                    rope_sum(b, 0)
                if embed:
                    x_stats(s, 1, par)
                if attend:
                    rope_sine(b, 1)
                if embed:
                    x_low(s, 0)
                    x_low(s, 1)
                if attend:
                    rope_sum(b, 1)
                    rope_sine(b, 2)
                if embed:
                    x_stats(s, 2, par)
                if attend:
                    rope_sum(b, 2)
                if embed:
                    y_evacuate(s, 0)
                    x_low(s, 2)
                if attend:
                    mask_scores(b, 0)
                if embed:
                    y_centre(s, 0)
                if attend:
                    mask_scores(b, 1)
                    sum_up(b, 0)
                if embed:
                    x_low(s, 3)
                    y_scale(s, 0)
                if attend:
                    turn_probs(b, 0)
                if embed:
                    h_stats(s, 0)
                if attend:
                    sum_up(b, 1)
                    mask_scores(b, 2)
                    turn_heads(b, 0)
                    turn_probs(b, 1)
                if embed:
                    x_low(s, 4)
                if attend:
                    mask_scores(b, 3)
                    sum_up(b, 2)
                    turn_heads(b, 1)
                if embed:
                    x_low(s, 5)
                if attend:
                    turn_probs(b, 2)
                if embed:
                    y_evacuate(s, 1)
                if attend:
                    turn_heads(b, 2)
                if embed:
                    y_centre(s, 1)
                if attend:
                    sum_up(b, 3)
                    add_attention(b, 0)
                    turn_probs(b, 3)
                if embed:
                    y_scale(s, 1)
                    h_stats(s, 1)
                if attend:
                    turn_heads(b, 3)
                    add_attention(b, 1)
                if embed:
                    y_evacuate(s, 2)
                if attend:
                    f_low(b, 0)
                if embed:
                    h_low(s, 0)
                if attend:
                    add_attention(b, 2)
                if embed:
                    y_centre(s, 2)
                if attend:
                    f_low(b, 1)
                if embed:
                    y_scale(s, 2)
                    h_stats(s, 2)
                if attend:
                    add_ffn(b, 0)
                    f_low(b, 2)
                if embed:
                    h_low(s, 1)
                    h_low(s, 2)
                if attend:
                    add_ffn(b, 1)
                    add_ffn(b, 2)

            def last_step():
                s, b = BATCHES, BATCHES - 1
                par_now[0] = s % 2
                rope_sine(b, 0)
                rope_sum(b, 0)
                rope_sine(b, 1)
                rope_sum(b, 1)
                rope_sine(b, 2)
                rope_sum(b, 2)
                mask_scores(b, 0)
                mask_scores(b, 1)
                sum_up(b, 0)
                turn_probs(b, 0)
                sum_up(b, 1)
                mask_scores(b, 2)
                turn_probs(b, 1)
                turn_heads(b, 0)
                sum_up(b, 2)
                mask_scores(b, 3)
                turn_heads(b, 1)
                turn_probs(b, 2)
                sum_up(b, 3)
                turn_heads(b, 2)
                turn_probs(b, 3)
                add_attention(b, 0)
                turn_heads(b, 3)
                add_attention(b, 1)
                f_low(b, 0)
                add_attention(b, 2)
                f_low(b, 1)
                add_ffn(b, 0)
                f_low(b, 2)
                add_ffn(b, 1)
                add_ffn(b, 2)

            first_step()
            run_steps(dve, step, last_step)


_INS = ["x", "W", "Wqkv", "Wo", "pweight", "nweight", "rows", "gates", "columns", "qkv_bias", "tables"]


def shape_tables():
    inv = 1.0 / 10000.0 ** (np.arange(HEAD // 2, dtype=np.float32) * 2.0 / HEAD)
    angle = inv.astype(np.float32)[:, None] * np.arange(SEQ, dtype=np.float32)[None, :]
    cos, sin = np.cos(angle), np.sin(angle)
    cos = np.tile(np.concatenate([cos, cos]), (P // Q, 1)).astype(np.float32)
    sin = np.tile(np.concatenate([-sin, sin]), (P // Q, 1)).astype(np.float32)
    query, key = np.arange(Q)[:, None], np.arange(SEQ)[None, :]
    causal = np.tile(np.where(key <= query, 0.0, NEG), (P // Q, 1)).astype(np.float32)
    return np.concatenate([cos, sin, causal], axis=1)


def kernel(**inputs):
    import concourse.bacc as _bacc
    from concourse.bass_utils import run_bass_kernel_spmd as _run

    nc = _bacc.Bacc("TRN2", target_bir_lowering=False, num_devices=1)
    arrays, args = {}, []
    a = {name: np.asarray(v) for name, v in inputs.items()}

    def columns(names):
        return [a[n].reshape(-1, P, *a[n].shape[1:]).swapaxes(0, 1).reshape(P, -1) for n in names]

    given = {
        "x": a["x"], "W": a["L0_tok_W"], "Wo": a["L0_attn_Wo"],
        "Wqkv": np.concatenate([a["L0_attn_Wk"], a["L0_attn_Wv"], a["L0_attn_Wq"]], axis=1),
        "pweight": a["L0_ffn_pweight"], "nweight": a["L0_ffn_nweight"],
        "rows": np.concatenate([a[n] for n in ROWS]),
        "gates": np.concatenate([a["L0_ffn_" + n] for n in ("exps", "bexps", "mask_weight", "scale", "biasscale")]),
        "columns": np.concatenate(columns(["L0_tok_g1", "L0_tok_b1", "L0_ffn_pbias", "L0_ffn_nbias"]), axis=1),
        "qkv_bias": np.concatenate(columns(["L0_attn_bk", "L0_attn_bv", "L0_attn_bq"]), axis=1),
        "tables": shape_tables(),
    }
    given = {name: np.ascontiguousarray(given[name]) for name in _INS}
    for name, a in given.items():
        arrays[f"in_{name}_dram"] = a
        args.append(nc.dram_tensor(f"in_{name}_dram", a.shape, mybir.dt.from_np(a.dtype), kind="ExternalInput").ap())
    args.append(nc.dram_tensor("out_0_dram", (SEQS, SEQ, HID), F32, kind="ExternalOutput").ap())
    audio_tower(nc, *args)
    r = _run(nc, [arrays], core_ids=[0])
    return r.results[0]["out_0_dram"]
```
